# Optimizing a Trainium2 kernel written in Bass

```python
import numpy as np
import jax
import jax.numpy as jnp

def _softmax(x, axis=-1):
    return jax.nn.softmax(x, axis=axis)

def _gelu(x):
    return jax.nn.gelu(x, approximate=True)

def _silu(x):
    return jax.nn.silu(x)

def _sigmoid(x):
    return jax.nn.sigmoid(x)

def _layernorm(x, axis=-1, eps=1e-05):
    m = jnp.mean(x, axis=axis, keepdims=True)
    v = jnp.var(x, axis=axis, keepdims=True)
    return (x - m) / jnp.sqrt(v + eps)

def _scatter_add(tgt, idx, src, axis=0):
    return tgt.at[idx].add(src)

def _segment_sum(src, seg, n):
    return jax.ops.segment_sum(src, seg, n)
kernel_name = 'mk_flamingo_gated_d1_seqx_r8_837994'

def setup_inputs(seed: int=0):
    np.random.seed(seed)
    _w = jnp.asarray

    def _rec_inputs():
        import jax
        import jax.numpy as jnp
        _rk = jax.random.key(seed)
        x = -0.0005207 + 1.001 * jax.random.normal(jax.random.fold_in(_rk, 1), (2, 256, 512), jnp.float32)
        _lenS = 256 - jax.random.randint(jax.random.fold_in(_rk, 7), (2,), 0, max(1, 256 // 4) + 1, jnp.int32)
        _lenS2 = 512 - jax.random.randint(jax.random.fold_in(_rk, 8), (2,), 0, max(1, 512 // 4) + 1, jnp.int32)
        _ctx_4096P = jax.random.normal(jax.random.fold_in(_rk, 11), (2, 16, 512), jnp.float32)
        _ctx_4096c = jax.random.dirichlet(jax.random.fold_in(_rk, 511), 0.3 * jnp.ones((16,), jnp.float32), (2, 512))
        _ctx_4096t = jnp.einsum('bsk,bkd->bsd', _ctx_4096c, _ctx_4096P)
        _ctx_4096t = _ctx_4096t * jax.lax.rsqrt(jnp.mean(jnp.square(_ctx_4096t)) + 1e-12) * 0.953939
        ctx_4096 = -0.00010331 + 0.999899 * (_ctx_4096t + 0.3 * jax.random.normal(jax.random.fold_in(_rk, 611), (2, 512, 512), jnp.float32))
        _g = jax.random.normal(jax.random.fold_in(_rk, 9001), (2, 1), jnp.float32)
        _g = jnp.sign(_g) * jnp.maximum(jnp.abs(_g), 1.0) + (_g == 0) * 1.0
        g_xattn = _g[0]
        g_ffn = _g[1]
        return (x, ctx_4096, g_xattn, g_ffn)
    x, ctx_4096, g_xattn, g_ffn = _rec_inputs()

    def _L0_xattn_setup():
        import jax, jax.numpy as jnp
        import numpy as np
        B, Q, D = (8, 64, 512)
        CTX = 512
        H, KV, HD = (16, 4, 96)
        G = H // KV
        key = jax.random.key(seed)
        ks = jax.random.split(key, 6)
        s = 0.02
        return {'latents': jax.random.normal(ks[0], (B, Q, D), jnp.float32), 'context': jax.random.normal(ks[1], (B, CTX, D), jnp.float32), 'Wq': jax.random.normal(ks[2], (H * HD, D), jnp.float32) * s, 'Wk': jax.random.normal(ks[3], (KV * HD, D), jnp.float32) * s, 'Wv': jax.random.normal(ks[4], (KV * HD, D), jnp.float32) * s, 'Wo': jax.random.normal(ks[5], (D, H * HD), jnp.float32) * s}
    _L0_xattn_all = _L0_xattn_setup()
    _L0_xattn_in = {k: v for k, v in _L0_xattn_all.items() if k in ('Wq', 'Wk', 'Wv', 'Wo')}
    del _L0_xattn_all

    def _L0_ffn_setup():
        import jax, jax.numpy as jnp
        import numpy as np
        BLOCK = 64
        NF4_CODE = jnp.array([-1.0, -0.6961928009986877, -0.5250730514526367, -0.39491748809814453, -0.28444138169288635, -0.18477343022823334, -0.09105003625154495, 0.0, 0.07958029955625534, 0.16093020141124725, 0.24611230194568634, 0.33791524171829224, 0.44070982933044434, 0.5626170039176941, 0.7229568362236023, 1.0], dtype=jnp.float32)

        def dequant_nf4(q, absmax, shape):
            w = NF4_CODE[q.reshape(-1)]
            w = w.reshape(-1, BLOCK) * absmax[:, None]
            return w.reshape(shape)
        key = jax.random.key(seed)
        ks = jax.random.split(key, 7)
        HD, M = (512, 1792)
        nblk = HD * M // BLOCK
        x = jax.random.normal(ks[0], (2, 256, HD), dtype=jnp.float32)
        gate_q = jax.random.randint(ks[1], (M, HD), 0, 16, dtype=jnp.int32)
        up_q = jax.random.randint(ks[2], (M, HD), 0, 16, dtype=jnp.int32)
        down_q = jax.random.randint(ks[3], (HD, M), 0, 16, dtype=jnp.int32)
        gate_absmax = jax.random.uniform(ks[4], (nblk,), dtype=jnp.float32) * 0.05
        up_absmax = jax.random.uniform(ks[5], (nblk,), dtype=jnp.float32) * 0.05
        down_absmax = jax.random.uniform(ks[6], (nblk,), dtype=jnp.float32) * 0.05
        return {'x': x, 'gate_q': gate_q, 'gate_absmax': gate_absmax, 'up_q': up_q, 'up_absmax': up_absmax, 'down_q': down_q, 'down_absmax': down_absmax}
    _L0_ffn_all = _L0_ffn_setup()
    _L0_ffn_in = {k: v for k, v in _L0_ffn_all.items() if k in ('gate_q', 'gate_absmax', 'up_q', 'up_absmax', 'down_q', 'down_absmax')}
    del _L0_ffn_all
    return {'x': x, 'ctx_4096': ctx_4096, 'g_xattn': g_xattn, 'g_ffn': g_ffn, 'L0_xattn_Wq': _L0_xattn_in['Wq'], 'L0_xattn_Wk': _L0_xattn_in['Wk'], 'L0_xattn_Wv': _L0_xattn_in['Wv'], 'L0_xattn_Wo': _L0_xattn_in['Wo'], 'L0_ffn_gate_q': _L0_ffn_in['gate_q'], 'L0_ffn_gate_absmax': _L0_ffn_in['gate_absmax'], 'L0_ffn_up_q': _L0_ffn_in['up_q'], 'L0_ffn_up_absmax': _L0_ffn_in['up_absmax'], 'L0_ffn_down_q': _L0_ffn_in['down_q'], 'L0_ffn_down_absmax': _L0_ffn_in['down_absmax']}

def reference(x, ctx_4096, g_xattn, g_ffn, L0_xattn_Wq, L0_xattn_Wk, L0_xattn_Wv, L0_xattn_Wo, L0_ffn_gate_q, L0_ffn_gate_absmax, L0_ffn_up_q, L0_ffn_up_absmax, L0_ffn_down_q, L0_ffn_down_absmax):
    import jax
    import jax.numpy as jnp

    def _L0_xattn_ref(latents, context, Wq, Wk, Wv, Wo):
        import jax, jax.numpy as jnp
        import numpy as np
        B, Q, D = (8, 64, 512)
        CTX = 512
        H, KV, HD = (16, 4, 96)
        G = H // KV
        b, q_len, _ = latents.shape
        hidden = jnp.concatenate([context, latents], axis=1)
        s_len = hidden.shape[1]
        q = (latents @ Wq.T).reshape(b, q_len, H, HD)
        k = (hidden @ Wk.T).reshape(b, s_len, KV, HD)
        v = (hidden @ Wv.T).reshape(b, s_len, KV, HD)
        q = q.transpose(0, 2, 1, 3).reshape(b, KV, G, q_len, HD)
        k = k.transpose(0, 2, 1, 3)
        v = v.transpose(0, 2, 1, 3)
        scale = 1.0 / jnp.sqrt(jnp.asarray(HD, q.dtype))
        scores = jnp.einsum('bkgqd,bksd->bkgqs', q, k) * scale
        attn = jax.nn.softmax(scores.astype(jnp.float32), axis=-1).astype(q.dtype)
        out = jnp.einsum('bkgqs,bksd->bkgqd', attn, v)
        out = out.reshape(b, H, q_len, HD).transpose(0, 2, 1, 3).reshape(b, q_len, H * HD)
        return out @ Wo.T

    def _L0_ffn_ref(x, gate_q, gate_absmax, up_q, up_absmax, down_q, down_absmax):
        import jax, jax.numpy as jnp
        import numpy as np
        BLOCK = 64
        NF4_CODE = jnp.array([-1.0, -0.6961928009986877, -0.5250730514526367, -0.39491748809814453, -0.28444138169288635, -0.18477343022823334, -0.09105003625154495, 0.0, 0.07958029955625534, 0.16093020141124725, 0.24611230194568634, 0.33791524171829224, 0.44070982933044434, 0.5626170039176941, 0.7229568362236023, 1.0], dtype=jnp.float32)

        def dequant_nf4(q, absmax, shape):
            w = NF4_CODE[q.reshape(-1)]
            w = w.reshape(-1, BLOCK) * absmax[:, None]
            return w.reshape(shape)
        HD = x.shape[-1]
        M = gate_q.shape[0]
        Wg = dequant_nf4(gate_q, gate_absmax, (M, HD))
        Wu = dequant_nf4(up_q, up_absmax, (M, HD))
        Wd = dequant_nf4(down_q, down_absmax, (HD, M))
        g = jnp.einsum('bsh,mh->bsm', x, Wg)
        u = jnp.einsum('bsh,mh->bsm', x, Wu)
        h = jax.nn.silu(g) * u
        return jnp.einsum('bsm,hm->bsh', h, Wd)
    x = x + jnp.tanh(g_xattn[0]) * _L0_xattn_ref(_layernorm(x, axis=-1), ctx_4096, L0_xattn_Wq, L0_xattn_Wk, L0_xattn_Wv, L0_xattn_Wo)
    x = x + jnp.tanh(g_ffn[0]) * _L0_ffn_ref(_layernorm(x, axis=-1), L0_ffn_gate_q, L0_ffn_gate_absmax, L0_ffn_up_q, L0_ffn_up_absmax, L0_ffn_down_q, L0_ffn_down_absmax)
    return x

_drawn_inputs = setup_inputs


def setup_inputs(seed=0):
    import zlib

    import numpy as np

    out = dict(_drawn_inputs(seed))
    spreads = {}
    factors = {'L0_xattn_Wq': 7.546,
     'L0_xattn_Wk': 7.464,
     'L0_ffn_gate_absmax': 3.205,
     'L0_ffn_up_absmax': 3.209,
     'L0_ffn_down_absmax': 3.228}
    for name, (base, spread) in spreads.items():
        noise = np.random.default_rng([zlib.crc32(name.encode()), seed]).standard_normal(out[name].shape)
        drawn = base * np.exp(spread * noise) if base else spread * noise
        out[name] = jnp.asarray(drawn.astype(out[name].dtype))
    for name, factor in factors.items():
        out[name] = (out[name] * factor).astype(out[name].dtype)
    return out
```

```python
from contextlib import ExitStack

import concourse.bass as bass
from concourse import mybir

P = 128
ROWS, D = 512, 512
RT, DC = ROWS // P, D // P
B, CTX, SEQ = 2, 512, 256
KEYS = CTX + SEQ
KT = KEYS // P
H, KV, HD = 16, 4, 96
G = H // KV
M = 1792
MT = M // P
BLOCK = 64
SCALE = float(HD) ** -0.5
EPS = 1e-5
TILES = H * RT
FW = 3 * D
HALF = FW // 2
CHUNKS = 2 * MT
OC = G * HD // P

F32 = mybir.dt.float32
F32R = mybir.dt.float32r
I32 = mybir.dt.int32
ALU = mybir.AluOpType
ACT = mybir.ActivationFunctionType
AX = mybir.AxisListType

NF4 = [-1.0, -0.6961928009986877, -0.5250730514526367, -0.39491748809814453, -0.28444138169288635,
       -0.18477343022823334, -0.09105003625154495, 0.0, 0.07958029955625534, 0.16093020141124725,
       0.24611230194568634, 0.33791524171829224, 0.44070982933044434, 0.5626170039176941,
       0.7229568362236023, 1.0]


def nf4_ramps():
    step = [NF4[i + 1] - NF4[i] for i in range(15)]
    slope = step[0]
    rest = [slope - s for s in step]
    ramps = []
    for left, full, right in ((1, 13, 14), (2, 3, 12), (4, 5, 11), (6, 9, 10), (7, 8, 9)):
        if (left, full) == (7, 8):
            left, full = None, 7
            right = 8
        w, z = rest[full], rest[right]
        x = rest[left] if left is not None else 0.0
        first = left + 1 if left is not None else full
        ramps.append((w, x - w * first, x + (right - first) * w + z))
        if left is not None:
            rest[left] = 0.0
        for i in range(first, right):
            rest[i] -= w
        rest[right] = 0.0
    return slope, -NF4[0], ramps


def misc_items():
    items = [(-1, "q", 0, 0)] + [(4 * h - 3, "q", h, 0) for h in range(1, H)]
    for g in range(KV):
        base = RT * G * (g + 1)
        at = (4, 6, 7, 8, 10, 11, 12) if g < KV - 1 else (3, 4, 5, 6, 7, 8, 9)
        items += [(base + at[c], "ot", g, c) for c in range(OC)]
        items += [(base + at[OC + r], "wo", g, r) for r in range(RT)]
    return sorted(items)


RAMPS = 2
TLAG, PLAG = 2, 3
ITERS = TILES + 10


def flamingo_block(nc, x, ctx_t, wkv_t, wq_t, wo_t, codes, absmax, g_xattn, g_ffn, weights, out):
    slope, offset, ramps = nf4_ramps()
    NR = len(ramps)
    MISC = misc_items()
    NM = {(k, i, p): n for n, (_, k, i, p) in enumerate(MISC)}
    Q_HI = {}
    n_hi = 0
    for n, (_, k, i, p) in enumerate(MISC):
        Q_HI[n] = n_hi
        n_hi += k != "wo"

    DEQ = {}
    for i in range(CHUNKS):
        DEQ.setdefault(2 + 2 * i, []).append(i)

    with ExitStack() as ctx:
        def sem(name):
            return ctx.enter_context(nc.semaphore(name))

        fixed, att_kv, early, att, ffn = (ExitStack() for _ in range(5))

        def sb(stack, name, shape, dt):
            return stack.enter_context(nc.sbuf_tensor(name, shape, dt))

        bank = ctx.enter_context(nc.psum_tensor("bank", [P, 8, 512], F32))

        xres = sb(fixed, "xres", [P, RT, D], F32)
        xT = [sb(fixed, f"xT_{s}", [P, DC, ROWS], F32R) for s in ("hi", "lo")]
        ident = sb(fixed, "ident", [P, P], F32)
        stats = sb(fixed, "stats", [P, RT, 6], F32)
        meanvar = sb(fixed, "meanvar", [P, RT, 2], F32)
        vareps = sb(fixed, "vareps", [P, RT], F32)
        neghalf = sb(fixed, "neghalf", [P, RT], F32)
        rough = sb(fixed, "rough", [P, RT], F32)
        newton = sb(fixed, "newton", [P, 2, RT], F32)
        rstd = sb(fixed, "rstd", [P, RT], F32)
        gates = sb(fixed, "gates", [P, 2], F32)
        gate_tanh = sb(fixed, "gate_tanh", [P, 2], F32)
        ramp_bias = sb(fixed, "ramp_bias", [P, NR], F32)
        negmax = sb(fixed, "negmax", [P, 4], F32)
        rowsum = sb(fixed, "rowsum", [P, TILES], F32)
        rinv = sb(fixed, "rinv", [P, TILES], F32)
        wq_raw = sb(fixed, "wq_raw", [P, 2, DC, HD], F32)
        wq = [sb(fixed, f"wq_{s}", [P, 2, DC, HD], F32R) for s in ("hi", "lo")]
        code_in = sb(fixed, "code_in", [P, 2, HALF], I32)
        scale_in = sb(fixed, "scale_in", [P, 2, HALF], F32)
        ramp = sb(fixed, "ramp", [P, RAMPS, HALF], F32)
        kT = [sb(att_kv, f"kT_{s}", [HD, KV, B, KEYS], F32R) for s in ("hi", "lo")]
        v = sb(att_kv, "v", [P, B * KT, KV, 2 * HD], F32R)
        wkv_raw = sb(early, "wkv_raw", [P, 2, 2 * KV * HD], F32)
        ctxT = [sb(early, f"ctxT_{s}", [P, DC, B * CTX], F32R) for s in ("hi", "lo")]
        wkv = [sb(early, f"wkv_{s}", [P, DC, 2 * KV * HD], F32R) for s in ("hi", "lo")]
        raw = ExitStack()
        ctx_raw = sb(raw, "ctx_raw", [P, 2, B * CTX], F32)
        raw.close()
        xhat = sb(early, "xhat", [P, RT, D], F32)
        early.close()
        qT = [sb(att, f"qT_{s}", [HD, 2, ROWS], F32R) for s in ("hi", "lo")]
        prob = sb(att, "prob", [P, 3, KEYS], F32)
        probT = [sb(att, f"probT_{s}", [P, 2, KEYS], F32R) for s in ("hi", "lo")]
        acc = sb(att, "acc", [P, HALF], F32)
        opart = sb(att, "opart", [P, HD], F32)
        og = sb(att, "og", [P, 2, RT, G * HD], F32)
        oT = [sb(att, f"oT_{s}", [P, OC, ROWS], F32R) for s in ("hi", "lo")]
        raw = ExitStack()
        wo_raw = sb(raw, "wo_raw", [P, OC, D], F32)
        raw.close()
        wo_lo_part = sb(att, "wo_lo", [P, OC, D], F32R)
        wo = [sb(att, "wo_hi", [P, OC, D], F32R), wo_lo_part]
        att.close()
        att_kv.close()
        wf_raw = sb(ffn, "wf_raw", [P, 2, FW], F32)
        wf = [sb(ffn, f"wf_{s}", [P, 3, FW], F32R) for s in ("hi", "lo")]
        sg = sb(ffn, "sg", [P, 2, ROWS], F32)
        hid = sb(ffn, "hid", [P, 2, ROWS], F32)
        hT = [sb(ffn, f"hT_{s}", [P, 2, ROWS], F32R) for s in ("hi", "lo")]
        xhat2 = sb(ffn, "xhat2", [P, RT, D], F32)
        result = xhat2
        ffn.close()
        fixed.close()

        x_in, g_in, wo_in = sem("x_in"), sem("g_in"), sem("wo_in")
        ctx_in, wkv_in = [[sem(f"{n}_in{i}") for i in range(DC)] for n in ("ctx", "wkv")]
        wq_in, code_at, scale_at, w_stored, wf_in = [
            [sem(f"{n}{i}") for i in range(2)] for n in ("wq_in", "code_at", "scale_at", "w_stored", "wf_in")]
        out_done = sem("out_done")
        const_done, zero_done = sem("const_done"), sem("zero_done")
        tanh_done = sem("tanh_done")
        ln_step, rough_step, xhat_done = sem("ln_step"), sem("rough_step"), sem("xhat_done")
        split_hi, split_lo = sem("split_hi"), sem("split_lo")
        unit_done, unit_hi, unit_lo = sem("unit_done"), sem("unit_hi"), sem("unit_lo")
        wq_hi, wq_lo, wo_hi, wo_lo = sem("wq_hi"), sem("wq_lo"), sem("wo_hi"), sem("wo_lo")
        scores_done, max_done, exp_done = sem("scores_done"), sem("max_done"), sem("exp_done")
        tr_done, pt_hi, pt_lo = sem("tr_done"), sem("pt_hi"), sem("pt_lo")
        pv_done, rinv_done, o_part, o_done = sem("pv_done"), sem("rinv_done"), sem("o_part"), sem("o_done")
        misc_done, misc_hi, misc_free = sem("misc_done"), sem("misc_hi"), sem("misc_free")
        line_step, ramp_done, ramp_used, w_ready = sem("line_step"), sem("ramp_done"), sem("ramp_used"), sem("w_ready")
        x2_done, x2_hi, x2_lo = sem("x2_done"), sem("x2_hi"), sem("x2_lo")
        wf_hi, wf_lo = sem("wf_hi"), sem("wf_lo")
        g_done, u_done, y_done = sem("g_done"), sem("u_done"), sem("y_done")
        sg_done, h_done, h_hi, h_lo, res_done = (
            sem("sg_done"), sem("h_done"), sem("h_hi"), sem("h_lo"), sem("res_done"))

        block = ctx.enter_context(nc.Block())

        V_CTX = [("v", t) for t in range(B * CTX // P)]
        K_CTX = [("k", h, b) for b in range(B) for h in range(KV)]
        X_T = [("x", c) for c in range(DC)]
        V_X = [("v", B * CTX // P + r) for r in range(RT)]
        K_X = [("k", h, B) for h in range(KV)]
        UNITS = V_CTX + K_CTX + X_T + V_X + K_X
        NU = len(UNITS)

        def unit_place(unit, u):
            if unit[0] == "v":
                t = unit[1]
                tile = (t // 4) * KT + t % 4 if t < 8 else ((t - 8) // 2) * KT + 4 + t % 2
                src = bank[:, u % 8, 0:KV * HD].rearrange("p (h d) -> p h d", h=KV)
                return src, v[:, tile, :, 0:HD], v[:, tile, :, HD:2 * HD]
            if unit[0] == "x":
                return bank[:, u % 8, :], xT[0][:, unit[1], :], xT[1][:, unit[1], :]
            _, h, b = unit
            if b < B:
                return (bank[0:HD, u % 8, :], kT[0][:, h, b, 0:CTX], kT[1][:, h, b, 0:CTX])
            src = bank[0:HD, u % 8, :].rearrange("p (b s) -> p b s", b=B)
            return src, kT[0][:, h, :, CTX:KEYS], kT[1][:, h, :, CTX:KEYS]

        def f32(ap):
            return ap.bitcast(F32)

        @block.sync
        def _(sp):
            for c in range(DC):
                if c >= 2:
                    sp.wait_ge(split_lo, 2 * (c - 1))
                sp.dma_start(ctx_raw[:, c % 2, :], ctx_t[c]).then_inc(ctx_in[c], 16)
                sp.dma_start(wkv_raw[:, c % 2, :], wkv_t[c]).then_inc(wkv_in[c], 16)
                if c == 1:
                    sp.dma_start(xres[:, :, :], x.rearrange("(r p) d -> p r d", p=P)).then_inc(x_in, 16)
                    sp.dma_start(gates[:, 0:1], g_xattn.to_broadcast([P, 1])).then_inc(g_in, 16)
                    sp.dma_start(gates[:, 1:2], g_ffn.to_broadcast([P, 1])).then_inc(g_in, 16)

            def load_wq(h):
                if h >= 2:
                    sp.wait_ge(wq_lo, h - 1)
                sp.dma_start(wq_raw[:, h % 2], wq_t[h].rearrange("p (c n) -> p c n", c=DC)).then_inc(wq_in[h % 2], 16)

            def load_chunk(i):
                if i >= 2:
                    sp.wait_ge(line_step, i - 1)
                    sp.wait_ge(ramp_done, NR * (i - 1))
                    sp.wait_ge(w_stored[i % 2], 16 * (i // 2))
                sp.dma_start(code_in[:, i % 2, :], codes[i // 2, :, bass.ts(i % 2, HALF)]).then_inc(code_at[i % 2], 16)
                for s in range(2):
                    sp.dma_start(scale_in[bass.ts(s, P // 2), i % 2, :],
                                 absmax[i // 2, s:s + 1, bass.ts(i % 2, HALF)].to_broadcast([P // 2, HALF])
                                 ).then_inc(scale_at[i % 2], 16)

            def store_chunk(i):
                sp.wait_ge(w_ready, i + 1)
                sp.dma_start(weights[i // 2, :, bass.ts(i % 2, HALF)], scale_in[:, i % 2, :]
                             ).then_inc(w_stored[i % 2], 16)

            load_wq(0)
            load_wq(1)
            load_chunk(0)
            load_chunk(1)
            for it in range(ITERS):
                if it % 4 == 0 and it // 4 + 2 < H:
                    load_wq(it // 4 + 2)
                if it % (RT * G) == 13 and it < TILES:
                    g = it // (RT * G)
                    if g == 0:
                        sp.wait_ge(unit_lo, NU)
                    else:
                        sp.wait_ge(misc_done, NM["wo", g - 1, RT - 1] + 1)
                    sp.dma_start(wo_raw[:, :, :], wo_t[g].rearrange("p (c n) -> p c n", c=OC)).then_inc(wo_in, 16)
                for i in DEQ.get(it - 1, []):
                    store_chunk(i)
                    if i + 2 < CHUNKS:
                        load_chunk(i + 2)
            for m in range(MT):
                if m == 0:
                    sp.wait_ge(pv_done, TILES)
                if m >= 2:
                    sp.wait_ge(wf_lo, m - 1)
                if m == 0:
                    for s in range(2):
                        sp.wait_ge(w_stored[s], 16 * MT)
                sp.dma_start(wf_raw[:, m % 2, :], weights[m]).then_inc(wf_in[m % 2], 16)
            for r in range(RT):
                sp.wait_ge(res_done, r + 1)
                sp.dma_start(out[bass.ts(r, P), :], result[:, r, :]).then_inc(out_done, 16)
            sp.wait_ge(out_done, 16 * RT)

        @block.tensor
        def _(pe):
            def three(o, a, b, first, last):
                pe.matmul(o, a[0], b[0], start=first, stop=False)
                pe.matmul(o, a[0], b[1], start=False, stop=False)
                return pe.matmul(o, a[1], b[0], start=False, stop=last)

            def both(pair, *idx):
                return [t[idx] for t in pair]

            ALL = slice(None)
            for c in range(DC):
                pe.wait_ge(split_lo, 2 * (c + 1))
                for u, (_, t) in enumerate(V_CTX):
                    mm = three(bank[:, u, 0:KV * HD], both(ctxT, ALL, c, bass.ts(t, P)),
                               both(wkv, ALL, c, slice(KV * HD, 2 * KV * HD)), c == 0, c == DC - 1)
                    if c == DC - 1:
                        mm.then_inc(unit_done, 1)
            for u in range(len(V_CTX), NU):
                unit = UNITS[u]
                pe.wait_ge(unit_lo, u - 7)
                if unit[0] == "x":
                    if unit[1] == 0:
                        pe.wait_ge(xhat_done, RT)
                        pe.wait_ge(const_done, 1)
                    for r in range(RT):
                        mm = pe.transpose(bank[:, u % 8, bass.ts(r, P)], xhat[:, r, bass.ts(unit[1], P)], ident[:, :])
                    mm.then_inc(unit_done, 1)
                    continue
                if u == len(V_CTX + K_CTX + X_T):
                    pe.wait_ge(unit_lo, u)
                for c in range(DC):
                    if unit[0] == "v":
                        mm = three(bank[:, u % 8, 0:KV * HD], both(xT, ALL, c, bass.ts(unit[1] - 8, P)),
                                   both(wkv, ALL, c, slice(KV * HD, 2 * KV * HD)), c == 0, c == DC - 1)
                    else:
                        _, h, b = unit
                        rhs = both(ctxT, ALL, c, bass.ts(b, CTX)) if b < B else both(xT, ALL, c, ALL)
                        mm = three(bank[0:HD, u % 8, :], both(wkv, ALL, c, bass.ts(h, HD)), rhs, c == 0, c == DC - 1)
                mm.then_inc(unit_done, 1)

            def misc(n):
                _, kind, i, part = MISC[n]
                if n:
                    pe.wait_ge(misc_free, n)
                else:
                    pe.wait_ge(unit_lo, NU - 4)
                o = bank[:, 7, :]
                if kind == "q":
                    pe.wait_ge(wq_lo, i + 1)
                    for c in range(DC):
                        mm = three(bank[0:HD, 7, :], both(wq, ALL, i % 2, c, ALL), both(xT, ALL, c, ALL),
                                   c == 0, c == DC - 1)
                elif kind == "ot":
                    if part == 0:
                        pe.wait_ge(o_done, RT * G * (i + 1))
                    for r in range(RT):
                        mm = pe.transpose(bank[:, 7, bass.ts(r, P)], og[:, i % 2, r, bass.ts(part, P)], ident[:, :])
                else:
                    if part == 0:
                        pe.wait_ge(wo_lo, i + 1)
                    for c in range(OC):
                        mm = three(o, both(oT, ALL, c, bass.ts(part, P)), both(wo, ALL, c, ALL), c == 0, c == OC - 1)
                mm.then_inc(misc_done, 1)

            def scores(t):
                h, r = divmod(t, RT)
                b, kv = r // 2, h // G
                if r == 0:
                    pe.wait_ge(misc_free, NM["q", h, 0] + 1)
                if t == 0:
                    pe.wait_ge(unit_lo, NU)
                if t >= 2:
                    pe.wait_ge(exp_done, t - 1)
                s = 2 * (t % 2)
                for o, keys in ((bank[:, s, :], slice(0, 512)), (bank[:, s + 1, 0:KEYS - 512], slice(512, KEYS))):
                    mm = three(o, both(qT, ALL, h % 2, bass.ts(r, P)), both(kT, ALL, kv, b, keys), True, True)
                mm.then_inc(scores_done, 1)

            def transposes(t):
                pe.wait_ge(exp_done, t + 1)
                for k in range(2):
                    n = 2 * t + k
                    if n >= 2:
                        pe.wait_ge(pt_lo, n - 1)
                    for j in range(3):
                        mm = pe.transpose(bank[:, 4 + k, bass.ts(j, P)],
                                          prob[:, t % 3, bass.ts(3 * k + j, P)], ident[:, :])
                    mm.then_inc(tr_done, 1)

            def values(t):
                h, r = divmod(t, RT)
                b, kv = r // 2, h // G
                if t:
                    pe.wait_ge(o_done, t)
                o = bank[:, 6, 0:2 * HD]
                for j in range(KT):
                    if j % 3 == 0:
                        pe.wait_ge(pt_lo, 2 * t + j // 3 + 1)
                    rhs = v[:, b * KT + j, kv, :]
                    pe.matmul(o, probT[0][:, t % 2, bass.ts(j, P)], rhs, start=(j == 0), stop=False)
                    mm = pe.matmul(o, probT[1][:, t % 2, bass.ts(j, P)], rhs, start=False, stop=(j == KT - 1))
                mm.then_inc(pv_done, 1)

            misc(0)
            for it in range(ITERS):
                if it < TILES:
                    scores(it)
                if 0 <= it - TLAG < TILES:
                    transposes(it - TLAG)
                if 0 <= it - PLAG < TILES:
                    values(it - PLAG)
                for n, item in enumerate(MISC):
                    if item[0] == it:
                        misc(n)

            for c in range(DC):
                if c == 0:
                    pe.wait_ge(xhat_done, 2 * RT)
                    pe.wait_ge(misc_free, len(MISC))
                for r in range(RT):
                    mm = pe.transpose(bank[:, 4 + c, bass.ts(r, P)], xhat2[:, r, bass.ts(c, P)], ident[:, :])
                mm.then_inc(x2_done, 1)

            def down(m):
                pe.wait_ge(h_lo, m + 1)
                for r in range(RT):
                    mm = three(bank[:, r, :], both(hT, ALL, m % 2, bass.ts(r, P)),
                               both(wf, ALL, m % 3, slice(2 * D, FW)), m == 0, m == MT - 1)
                    if m == MT - 1:
                        mm.then_inc(y_done, 1)
                if m < MT - 1:
                    mm.then_inc(y_done, 1)

            for m in range(MT):
                pe.wait_ge(wf_lo, m + 1)
                if m == 0:
                    pe.wait_ge(x2_lo, DC)
                if m >= 2:
                    pe.wait_ge(h_done, m - 1)
                for k, done in ((0, g_done), (1, u_done)):
                    for c in range(DC):
                        mm = three(bank[:, 4 + 2 * (m % 2) + k, :], both(wf, ALL, m % 3, bass.ts(4 * k + c, P)),
                                   both(xT, ALL, c, ALL), c == 0, c == DC - 1)
                    mm.then_inc(done, 1)
                if m:
                    down(m - 1)
            down(MT - 1)

        @block.scalar
        def _(act):
            act.wait_ge(g_in, 32)
            act.activation(gate_tanh[:, :], gates[:, :], ACT.Tanh).then_inc(tanh_done, 1)
            for c in range(DC):
                act.wait_ge(ctx_in[c], 16)
                act.copy(ctxT[0][:, c, :], ctx_raw[:, c % 2, :]).then_inc(split_hi, 1)
                act.wait_ge(wkv_in[c], 16)
                act.copy(wkv[0][:, c, :], wkv_raw[:, c % 2, :]).then_inc(split_hi, 1)
            for u, unit in enumerate(UNITS):
                src, hi, _ = unit_place(unit, u)
                act.wait_ge(unit_done, u + 1)
                act.copy(hi, src).then_inc(unit_hi, 1)

            def misc(n):
                _, kind, i, part = MISC[n]
                if kind == "wo":
                    return
                act.wait_ge(misc_done, n + 1)
                if kind == "q":
                    if n == 0:
                        act.wait_ge(unit_lo, NU)
                    act.mul(qT[0][:, i % 2, :], bank[0:HD, 7, :], SCALE).then_inc(misc_hi, 1)
                else:
                    act.copy(oT[0][:, part, :], bank[:, 7, :]).then_inc(misc_hi, 1)

            def dequant_ramps(i):
                act.wait_ge(code_at[i % 2], 16 * (i // 2 + 1))
                if i == 0:
                    act.wait_ge(const_done, 1)
                for j, (w, _, _) in enumerate(ramps):
                    n = NR * i + j
                    if n >= RAMPS:
                        act.wait_ge(ramp_used, n - RAMPS + 1)
                    act.activation(ramp[:, n % RAMPS, :], code_in[:, i % 2, :], ACT.Relu, bias=ramp_bias[:, j:j + 1],
                                   scale=w).then_inc(ramp_done, 1)

            misc(0)
            for it in range(ITERS):
                if 0 <= it - TLAG < TILES:
                    t = it - TLAG
                    for k in range(2):
                        act.wait_ge(tr_done, 2 * t + k + 1)
                        if k == 0 and t >= 2:
                            act.wait_ge(pv_done, t - 1)
                        act.copy(probT[0][:, t % 2, bass.ts(k, 384)], bank[:, 4 + k, 0:384]).then_inc(pt_hi, 1)
                if it < TILES:
                    act.wait_ge(max_done, it + 1)
                    if it >= 3:
                        act.wait_ge(tr_done, 2 * (it - 2))
                    s = 2 * (it % 2)
                    act.activation(prob[:, it % 3, :], bank[:, s:s + 2, :].rearrange("p a n -> p (a n)")[:, 0:KEYS],
                                   ACT.Exp, bias=negmax[:, it % 4:it % 4 + 1],
                                   accum_out=rowsum[:, it:it + 1]).then_inc(exp_done, 1)
                if 0 <= it - PLAG < TILES:
                    t = it - PLAG
                    act.wait_ge(pv_done, t + 1)
                    act.wait_ge(rinv_done, t + 1)
                    if t:
                        act.wait_ge(o_done, t)
                    act.mul(opart[:, :], bank[:, 6, HD:2 * HD], rinv[:, t:t + 1]).then_inc(o_part, 1)
                for n, item in enumerate(MISC):
                    if item[0] == it:
                        misc(n)
                for i in DEQ.get(it, []):
                    dequant_ramps(i)

            def split_wf(m):
                act.wait_ge(wf_in[m % 2], 16 * (m // 2 + 1))
                if m >= 3:
                    act.wait_ge(y_done, m - 2)
                act.copy(wf[0][:, m % 3, :], wf_raw[:, m % 2, :]).then_inc(wf_hi, 1)

            split_wf(0)
            for c in range(DC):
                act.wait_ge(x2_done, c + 1)
                act.copy(xT[0][:, c, :], bank[:, 4 + c, :]).then_inc(x2_hi, 1)
            split_wf(1)
            for m in range(MT):
                act.wait_ge(g_done, m + 1)
                if m >= 2:
                    act.wait_ge(h_done, m - 1)
                act.activation(sg[:, m % 2, :], bank[:, 4 + 2 * (m % 2), :], ACT.Silu, scale=-1.0).then_inc(sg_done, 1)
                if m + 2 < MT:
                    split_wf(m + 2)

        @block.vector
        def _(dve):
            ln_count = [0]

            def link(ins):
                ln_count[0] += 1
                ins.then_inc(ln_step, 1)
                dve.wait_ge(ln_step, ln_count[0])

            def layer_norm(dst, n):
                for r in range(RT):
                    ins = dve.bn_stats(stats[:, r, :], xres[:, r, :])
                link(ins)
                for r in range(RT):
                    ins = dve.bn_aggr(meanvar[:, r, :], stats[:, r, :])
                link(ins)
                link(dve.tensor_scalar(vareps[:, :], meanvar[:, :, 1], EPS, None, ALU.add))
                ln_ready.append(ln_count[0])
                dve.wait_ge(rough_step, n + 1)
                link(dve.tensor_tensor(newton[:, 0, :], rough[:, :], rough[:, :], ALU.mult))
                link(dve.scalar_tensor_tensor(out=newton[:, 1, :], in0=newton[:, 0, :], scalar=-0.5, in1=vareps[:, :],
                                              op0=ALU.mult, op1=ALU.mult))
                link(dve.scalar_tensor_tensor(out=rstd[:, :], in0=newton[:, 1, :], scalar=1.5, in1=rough[:, :],
                                              op0=ALU.add, op1=ALU.mult))
                for r in range(RT):
                    dve.tensor_scalar(dst[:, r, :], xres[:, r, :], meanvar[:, r, 0:1], rstd[:, r:r + 1],
                                      ALU.subtract, ALU.mult).then_inc(xhat_done, 1)

            ln_ready = []
            for j, (_, b, _) in enumerate(ramps):
                ins = dve.memset(ramp_bias[:, j:j + 1], b)
            dve.memset(neghalf[:, :], -0.5).then_inc(zero_done, 1)
            for c in range(DC):
                dve.wait_ge(split_hi, 2 * c + 1)
                dve.tensor_tensor(ctxT[1][:, c, :], ctx_raw[:, c % 2, :], f32(ctxT[0][:, c, :]),
                                  ALU.subtract).then_inc(split_lo, 1)
                dve.wait_ge(split_hi, 2 * c + 2)
                dve.tensor_tensor(wkv[1][:, c, :], wkv_raw[:, c % 2, :], f32(wkv[0][:, c, :]),
                                  ALU.subtract).then_inc(split_lo, 1)

            def split_wq(h):
                dve.wait_ge(wq_in[h % 2], 16 * (h // 2 + 1))
                if h >= 2:
                    dve.wait_ge(misc_done, NM["q", h - 2, 0] + 1)
                dve.tensor_copy(wq[0][:, h % 2], wq_raw[:, h % 2]).then_inc(wq_hi, 1)

            for u, unit in enumerate(UNITS):
                if u == 8:
                    dve.wait_ge(x_in, 16)
                    layer_norm(xhat, 0)
                    split_wq(0)
                    split_wq(1)
                src, hi, lo = unit_place(unit, u)
                dve.wait_ge(unit_hi, u + 1)
                dve.tensor_tensor(lo, src, f32(hi), ALU.subtract).then_inc(unit_lo, 1)

            def misc(n):
                _, kind, i, part = MISC[n]
                if kind == "wo":
                    if (i, part) == (0, 0):
                        dve.wait_ge(tanh_done, 1)
                    dve.wait_ge(misc_done, n + 1)
                    dve.scalar_tensor_tensor(out=xres[:, part, :], in0=bank[:, 7, :], scalar=gate_tanh[:, 0:1],
                                             in1=xres[:, part, :], op0=ALU.mult, op1=ALU.add).then_inc(misc_free, 1)
                    return
                dve.wait_ge(misc_hi, Q_HI[n] + 1)
                if kind == "q":
                    dve.scalar_tensor_tensor(out=qT[1][:, i % 2, :], in0=bank[0:HD, 7, :], scalar=SCALE,
                                             in1=f32(qT[0][:, i % 2, :]), op0=ALU.mult,
                                             op1=ALU.subtract).then_inc(misc_free, 1)
                else:
                    dve.tensor_tensor(oT[1][:, part, :], bank[:, 7, :], f32(oT[0][:, part, :]),
                                      ALU.subtract).then_inc(misc_free, 1)

            def dequant_sum(i):
                a = acc[:, :]
                dve.wait_ge(code_at[i % 2], 16 * (i // 2 + 1))
                if i:
                    dve.wait_ge(w_ready, i)
                dve.tensor_scalar(a, code_in[:, i % 2, :], -slope, offset, ALU.mult, ALU.add).then_inc(line_step, 1)
                for j, (_, _, c) in enumerate(ramps):
                    dve.wait_ge(ramp_done, NR * i + j + 1)
                    if j == 0:
                        dve.wait_ge(line_step, i + 1)
                    else:
                        dve.wait_ge(ramp_used, NR * i + j)
                    ins = dve.scalar_tensor_tensor(out=a, in0=ramp[:, (NR * i + j) % RAMPS, :], scalar=c, in1=a, op0=ALU.min,
                                                   op1=ALU.add)
                    ins.then_inc(ramp_used, 1)

            misc(0)
            for it in range(ITERS):
                if it < TILES:
                    s = 2 * (it % 2)
                    dve.wait_ge(scores_done, it + 1)
                    if it >= 4:
                        dve.wait_ge(exp_done, it - 3)
                    dve.tensor_reduce(negmax[:, it % 4:it % 4 + 1],
                                      bank[:, s:s + 2, :].rearrange("p a n -> p (a n)")[:, 0:KEYS],
                                      AX.X, ALU.max, negate=True).then_inc(max_done, 1)
                if 0 <= it - TLAG < TILES:
                    t = it - TLAG
                    for k in range(2):
                        dve.wait_ge(pt_hi, 2 * t + k + 1)
                        dve.tensor_tensor(probT[1][:, t % 2, bass.ts(k, 384)], bank[:, 4 + k, 0:384],
                                          f32(probT[0][:, t % 2, bass.ts(k, 384)]), ALU.subtract).then_inc(pt_lo, 1)
                    dve.wait_ge(exp_done, t + 1)
                    dve.reciprocal(rinv[:, t:t + 1], rowsum[:, t:t + 1]).then_inc(rinv_done, 1)
                if 0 <= it - PLAG < TILES:
                    t = it - PLAG
                    h, r = divmod(t, RT)
                    g = h // G
                    dve.wait_ge(o_part, t + 1)
                    if r == 0 and h % G == 0 and g >= 2:
                        dve.wait_ge(misc_done, NM["ot", g - 2, OC - 1] + 1)
                    dve.wait_ge(rinv_done, t + 1)
                    dve.scalar_tensor_tensor(out=og[:, g % 2, r, bass.ts(h % G, HD)], in0=bank[:, 6, 0:HD],
                                             scalar=rinv[:, t:t + 1], in1=opart[:, :], op0=ALU.mult,
                                             op1=ALU.add).then_inc(o_done, 1)
                for n, item in enumerate(MISC):
                    if item[0] == it:
                        misc(n)
                if it % 4 == 2 and it // 4 + 2 < H:
                    split_wq(it // 4 + 2)
                if it >= RT * G and it % (RT * G) == 2:
                    dve.wait_ge(wo_in, it // G // RT * 16)
                    dve.tensor_copy(wo[0][:, :, :], wo_raw[:, :, :]).then_inc(wo_hi, 1)
                for i in DEQ.get(it, []):
                    dequant_sum(i)

            dve.wait_ge(misc_free, len(MISC))
            layer_norm(xhat2, 1)
            for c in range(DC):
                dve.wait_ge(x2_hi, c + 1)
                dve.tensor_tensor(xT[1][:, c, :], bank[:, 4 + c, :], f32(xT[0][:, c, :]),
                                  ALU.subtract).then_inc(x2_lo, 1)
            for m in range(MT):
                dve.wait_ge(u_done, m + 1)
                dve.wait_ge(sg_done, m + 1)
                dve.tensor_tensor(hid[:, m % 2, :], bank[:, 5 + 2 * (m % 2), :], sg[:, m % 2, :],
                                  ALU.mult).then_inc(h_done, 1)
                dve.wait_ge(h_done, m + 1)
                if m >= 2:
                    dve.wait_ge(y_done, m - 1)
                dve.tensor_copy(hT[0][:, m % 2, :], hid[:, m % 2, :]).then_inc(h_hi, 1)
                dve.wait_ge(h_hi, m + 1)
                dve.tensor_tensor(hT[1][:, m % 2, :], hid[:, m % 2, :], f32(hT[0][:, m % 2, :]),
                                  ALU.subtract).then_inc(h_lo, 1)
            for r in range(RT):
                dve.wait_ge(y_done, MT + r)
                dve.scalar_tensor_tensor(out=result[:, r, :], in0=bank[:, r, :], scalar=gate_tanh[:, 1:2],
                                         in1=xres[:, r, :], op0=ALU.mult, op1=ALU.add).then_inc(res_done, 1)

        @block.gpsimd
        def _(pool):
            pool.memset(ident[:, :], 0.0).then_inc(zero_done, 1)
            pool.wait_ge(zero_done, 2)
            pool.affine_select(out=ident[:, :], in_=ident[:, :], compare_op=ALU.not_equal, fill=1.0, base=0,
                               pattern=[[-1, P]], channel_multiplier=1).then_inc(const_done, 1)

            def rough_power(n):
                pool.wait_ge(ln_step, 3 + 6 * n)
                pool.tensor_tensor(rough[:, :], vareps[:, :], neghalf[:, :], ALU.pow).then_inc(rough_step, 1)

            def split_wq(h):
                pool.wait_ge(wq_hi, h + 1)
                pool.tensor_tensor(wq[1][:, h % 2], wq_raw[:, h % 2], f32(wq[0][:, h % 2]),
                                   ALU.subtract).then_inc(wq_lo, 1)

            rough_power(0)
            split_wq(0)
            split_wq(1)
            for it in range(ITERS):
                if it % 4 == 2 and it // 4 + 2 < H:
                    split_wq(it // 4 + 2)
                if it >= RT * G and it % (RT * G) == 2:
                    pool.wait_ge(wo_hi, it // (RT * G))
                    pool.tensor_tensor(wo[1][:, :, :], wo_raw[:, :, :], f32(wo[0][:, :, :]),
                                       ALU.subtract).then_inc(wo_lo, 1)
                for i in DEQ.get(it, []):
                    pool.wait_ge(scale_at[i % 2], 32 * (i // 2 + 1))
                    pool.wait_ge(ramp_used, NR * (i + 1))
                    pool.tensor_tensor(scale_in[:, i % 2, :], acc[:, :], scale_in[:, i % 2, :],
                                       ALU.mult).then_inc(w_ready, 1)
            rough_power(1)
            for m in range(MT):
                pool.wait_ge(wf_hi, m + 1)
                pool.tensor_tensor(wf[1][:, m % 3, :], wf_raw[:, m % 2, :], f32(wf[0][:, m % 3, :]),
                                   ALU.subtract).then_inc(wf_lo, 1)


def kernel(**inputs):
    import numpy as np
    import concourse.bacc as bacc
    from concourse.bass_utils import run_bass_kernel_spmd

    a = {k: np.asarray(x) for k, x in inputs.items()}

    def tiles_of(w):
        return w.T.reshape(DC, P, MT, P).transpose(2, 1, 0, 3).reshape(MT, P, DC * P)

    def scales_of(s):
        return s.reshape(MT, P, DC, 2).transpose(0, 3, 2, 1).reshape(MT, 2, DC * P)

    arrays = {
        "x": a["x"].reshape(ROWS, D),
        "ctx_t": a["ctx_4096"].reshape(B * CTX, D).T.reshape(DC, P, B * CTX),
        "wkv_t": np.concatenate([a["L0_xattn_Wk"].T, a["L0_xattn_Wv"].T], axis=1).reshape(DC, P, 2 * KV * HD),
        "wq_t": a["L0_xattn_Wq"].T.reshape(DC, P, H, HD).transpose(2, 1, 0, 3).reshape(H, P, DC * HD),
        "wo_t": a["L0_xattn_Wo"].T.reshape(KV, OC, P, D).transpose(0, 2, 1, 3).reshape(KV, P, OC * D),
        "codes": np.concatenate([
            tiles_of(a["L0_ffn_gate_q"]), tiles_of(a["L0_ffn_up_q"]),
            a["L0_ffn_down_q"].T.reshape(MT, P, D)], axis=2),
        "absmax": np.concatenate([
            scales_of(a["L0_ffn_gate_absmax"]), scales_of(a["L0_ffn_up_absmax"]),
            a["L0_ffn_down_absmax"].reshape(D, MT, 2).transpose(1, 2, 0)], axis=2),
        "g_xattn": a["g_xattn"].reshape(1, 1),
        "g_ffn": a["g_ffn"].reshape(1, 1),
    }
    nc = bacc.Bacc("TRN2", target_bir_lowering=False, num_devices=1)
    arrays = {k: np.ascontiguousarray(x) for k, x in arrays.items()}
    args = [nc.dram_tensor(f"in_{k}", x.shape, mybir.dt.from_np(x.dtype), kind="ExternalInput").ap()
            for k, x in arrays.items()]
    weights = nc.dram_tensor("ffn_weights", (MT, P, FW), F32, kind="Internal").ap()
    out = nc.dram_tensor("out", (ROWS, D), F32, kind="ExternalOutput").ap()
    flamingo_block(nc, *args, weights, out)
    r = run_bass_kernel_spmd(nc, [{f"in_{k}": x for k, x in arrays.items()}], core_ids=[0])
    return r.results[0]["out"].reshape(B, SEQ, D)
```

```python
from contextlib import ExitStack

import concourse.bass as bass
from concourse import mybir

P = 128
ROWS, D = 512, 512
RT, DC = ROWS // P, D // P
B, CTX, SEQ = 2, 512, 256
KEYS = CTX + SEQ
KT = KEYS // P
H, KV, HD = 16, 4, 96
G = H // KV
M = 1792
MT = M // P
BLOCK = 64
SCALE = float(HD) ** -0.5
EPS = 1e-5
TILES = H * RT
FW = 3 * D
HALF = FW // 2
CHUNKS = 2 * MT
OC = G * HD // P

F32 = mybir.dt.float32
F32R = mybir.dt.float32r
I32 = mybir.dt.int32
ALU = mybir.AluOpType
ACT = mybir.ActivationFunctionType
AX = mybir.AxisListType

NF4 = [-1.0, -0.6961928009986877, -0.5250730514526367, -0.39491748809814453, -0.28444138169288635,
       -0.18477343022823334, -0.09105003625154495, 0.0, 0.07958029955625534, 0.16093020141124725,
       0.24611230194568634, 0.33791524171829224, 0.44070982933044434, 0.5626170039176941,
       0.7229568362236023, 1.0]


def nf4_ramps():
    step = [NF4[i + 1] - NF4[i] for i in range(15)]
    slope = step[0]
    rest = [slope - s for s in step]
    ramps = []
    for left, full, right in ((1, 13, 14), (2, 3, 12), (4, 5, 11), (6, 9, 10), (7, 8, 9)):
        if (left, full) == (7, 8):
            left, full = None, 7
            right = 8
        w, z = rest[full], rest[right]
        x = rest[left] if left is not None else 0.0
        first = left + 1 if left is not None else full
        ramps.append((w, x - w * first, x + (right - first) * w + z))
        if left is not None:
            rest[left] = 0.0
        for i in range(first, right):
            rest[i] -= w
        rest[right] = 0.0
    return slope, -NF4[0], ramps


def misc_items():
    items = [(-1, "q", 0, 0)] + [(4 * h - 3, "q", h, 0) for h in range(1, H)]
    for g in range(KV):
        if g == KV - 1:
            break
        base = RT * G * (g + 1)
        at = (4, 6, 7, 8, 10, 11, 12)
        items += [(base + at[c], "ot", g, c) for c in range(OC)]
        items += [(base + at[OC + r], "wo", g, r) for r in range(RT)]
    return sorted(items)


RAMPS = 2
TAIL = (4, 5, 7)
TLAG, PLAG = 2, 3
ITERS = TILES + PLAG
STEPS = 5
LEAD = 1


UNIT0 = 9


def dequant_slots(units):
    slots, n = {}, 0
    places = [(("unit", u), 1) for u in range(UNIT0, units)]
    places += [(("att", it), 2 if it % 8 == 1 else 1) for it in range(TILES)]
    places += [(("ffn", m), 5) for m in range(MT)]
    for place, k in places:
        slots[place] = list(range(n, min(n + k, CHUNKS * STEPS)))
        n += len(slots[place])
    assert n == CHUNKS * STEPS
    made, k = {}, 0
    for place, _ in places:
        made[place] = [j for j in range(k, min(max(slots[place], default=n) + LEAD + 1, n))]
        k += len(made[place])
    return slots, made


def flamingo_block(nc, x, ctx_t, wkv_t, wq_t, wo_t, codes, absmax, g_xattn, g_ffn, weights, out):
    slope, offset, ramps = nf4_ramps()
    NR = len(ramps)
    MISC = misc_items()
    NM = {(k, i, p): n for n, (_, k, i, p) in enumerate(MISC)}
    Q_HI = {}
    n_hi = 0
    for n, (_, k, i, p) in enumerate(MISC):
        Q_HI[n] = n_hi
        n_hi += k != "wo"

    with ExitStack() as ctx:
        def sem(name):
            return ctx.enter_context(nc.semaphore(name))

        fixed, att_kv, early, att, ffn = (ExitStack() for _ in range(5))

        def sb(stack, name, shape, dt):
            return stack.enter_context(nc.sbuf_tensor(name, shape, dt))

        bank = ctx.enter_context(nc.psum_tensor("bank", [P, 8, 512], F32))

        xres = sb(fixed, "xres", [P, RT, D], F32)
        xT = [sb(fixed, f"xT_{s}", [P, DC, ROWS], F32R) for s in ("hi", "lo")]
        ident = sb(fixed, "ident", [P, P], F32)
        stats = sb(fixed, "stats", [P, RT, 6], F32)
        meanvar = sb(fixed, "meanvar", [P, RT, 2], F32)
        vareps = sb(fixed, "vareps", [P, RT], F32)
        neghalf = sb(fixed, "neghalf", [P, RT], F32)
        rough = sb(fixed, "rough", [P, RT], F32)
        newton = sb(fixed, "newton", [P, 2, RT], F32)
        rstd = sb(fixed, "rstd", [P, RT], F32)
        gates = sb(fixed, "gates", [P, 2], F32)
        gate_tanh = sb(fixed, "gate_tanh", [P, 2], F32)
        ramp_bias = sb(fixed, "ramp_bias", [P, NR], F32)
        negmax = sb(fixed, "negmax", [P, 4], F32)
        rowsum = sb(fixed, "rowsum", [P, TILES], F32)
        rinv = sb(fixed, "rinv", [P, TILES], F32)
        wq_raw = sb(fixed, "wq_raw", [P, 2, DC, HD], F32)
        wq = [sb(fixed, f"wq_{s}", [P, 2, DC, HD], F32R) for s in ("hi", "lo")]
        code_in = sb(fixed, "code_in", [P, 2, HALF], I32)
        scale_in = sb(fixed, "scale_in", [P, 2, HALF], F32)
        acc = sb(fixed, "acc", [P, 2, HALF], F32)
        ramp = sb(fixed, "ramp", [P, RAMPS, HALF], F32)
        kT = [sb(att_kv, f"kT_{s}", [HD, KV, B, KEYS], F32R) for s in ("hi", "lo")]
        v = sb(att_kv, "v", [P, B * KT, KV, 2 * HD], F32R)
        wkv_raw = sb(early, "wkv_raw", [P, 2, 2 * KV * HD], F32)
        ctxT = [sb(early, f"ctxT_{s}", [P, DC, B * CTX], F32R) for s in ("hi", "lo")]
        wkv = [sb(early, f"wkv_{s}", [P, DC, 2 * KV * HD], F32R) for s in ("hi", "lo")]
        raw = ExitStack()
        ctx_raw = sb(raw, "ctx_raw", [P, DC, B * CTX], F32)
        raw.close()
        xhat = sb(early, "xhat", [P, RT, D], F32)
        early.close()
        qT = [sb(att, f"qT_{s}", [HD, 2, ROWS], F32R) for s in ("hi", "lo")]
        prob = sb(att, "prob", [P, 3, KEYS], F32)
        probT = [sb(att, f"probT_{s}", [P, 2, KEYS], F32R) for s in ("hi", "lo")]
        opart = sb(att, "opart", [P, HD], F32)
        og = sb(att, "og", [P, 2, RT, G * HD], F32)
        oT = [sb(att, f"oT_{s}", [P, OC, ROWS], F32R) for s in ("hi", "lo")]
        raw = ExitStack()
        wo_raw = sb(raw, "wo_raw", [P, OC, D], F32)
        raw.close()
        wo_lo_part = sb(att, "wo_lo", [P, OC, D], F32R)
        wo = [sb(att, "wo_hi", [P, OC, D], F32R), wo_lo_part]
        att.close()
        att_kv.close()
        wf_raw = sb(ffn, "wf_raw", [P, 2, FW], F32)
        wf = [sb(ffn, f"wf_{s}", [P, 3, FW], F32R) for s in ("hi", "lo")]
        sg = sb(ffn, "sg", [P, 2, ROWS], F32)
        hid = sb(ffn, "hid", [P, 2, ROWS], F32)
        hT = [sb(ffn, f"hT_{s}", [P, 2, ROWS], F32R) for s in ("hi", "lo")]
        xhat2 = sb(ffn, "xhat2", [P, RT, D], F32)
        result = xhat2
        ffn.close()
        fixed.close()

        x_in, g_in, wo_in = sem("x_in"), sem("g_in"), sem("wo_in")
        ctx_in, wkv_in = [[sem(f"{n}_in{i}") for i in range(DC)] for n in ("ctx", "wkv")]
        wq_in, code_at, scale_at, w_stored, wf_in = [
            [sem(f"{n}{i}") for i in range(2)] for n in ("wq_in", "code_at", "scale_at", "w_stored", "wf_in")]
        out_done = sem("out_done")
        const_done, zero_done = sem("const_done"), sem("zero_done")
        tanh_done = sem("tanh_done")
        ln_step, var_done, rough_done, xhat_done = sem("ln_step"), sem("var_done"), sem("rough_done"), sem("xhat_done")
        split_hi, split_lo = sem("split_hi"), sem("split_lo")
        unit_done, unit_hi, unit_lo = sem("unit_done"), sem("unit_hi"), sem("unit_lo")
        wq_hi, wq_lo, wo_hi, wo_lo = sem("wq_hi"), sem("wq_lo"), sem("wo_hi"), sem("wo_lo")
        scores_done, max_done, exp_done = sem("scores_done"), sem("max_done"), sem("exp_done")
        tr_done, pt_hi, pt_lo = sem("tr_done"), sem("pt_hi"), sem("pt_lo")
        pv_done, rinv_done, o_part, o_done = sem("pv_done"), sem("rinv_done"), sem("o_part"), sem("o_done")
        misc_done, misc_hi, misc_free = sem("misc_done"), sem("misc_hi"), sem("misc_free")
        tail_done, tail_hi, tail_lo, rows_done = sem("tail_done"), sem("tail_hi"), sem("tail_lo"), sem("rows_done")
        line_step, ramp_done, ramp_used, w_ready = sem("line_step"), sem("ramp_done"), sem("ramp_used"), sem("w_ready")
        x2_done, x2_hi, x2_lo = sem("x2_done"), sem("x2_hi"), sem("x2_lo")
        wf_hi, wf_lo = sem("wf_hi"), sem("wf_lo")
        g_done, u_done, y_done = sem("g_done"), sem("u_done"), sem("y_done")
        sg_done, h_done, h_hi, h_lo, res_done = (
            sem("sg_done"), sem("h_done"), sem("h_hi"), sem("h_lo"), sem("res_done"))

        block = ctx.enter_context(nc.Block())

        V_CTX = [("v", t) for t in range(B * CTX // P)]
        K_CTX = [("k", h, b) for b in range(B) for h in range(KV)]
        X_T = [("x", c) for c in range(DC)]
        V_X = [("v", B * CTX // P + r) for r in range(RT)]
        K_X = [("k", h, B) for h in range(KV)]
        UNITS = V_CTX + K_CTX + X_T + V_X + K_X
        NU = len(UNITS)
        SLOTS, MADE = dequant_slots(NU)

        def unit_place(unit, u):
            if unit[0] == "v":
                t = unit[1]
                tile = (t // 4) * KT + t % 4 if t < 8 else ((t - 8) // 2) * KT + 4 + t % 2
                src = bank[:, u % 8, 0:KV * HD].rearrange("p (h d) -> p h d", h=KV)
                return src, v[:, tile, :, 0:HD], v[:, tile, :, HD:2 * HD]
            if unit[0] == "x":
                return bank[:, u % 8, :], xT[0][:, unit[1], :], xT[1][:, unit[1], :]
            _, h, b = unit
            if b < B:
                return (bank[0:HD, u % 8, :], kT[0][:, h, b, 0:CTX], kT[1][:, h, b, 0:CTX])
            src = bank[0:HD, u % 8, :].rearrange("p (b s) -> p b s", b=B)
            return src, kT[0][:, h, :, CTX:KEYS], kT[1][:, h, :, CTX:KEYS]

        def f32(ap):
            return ap.bitcast(F32)

        @block.sync
        def _(sp):
            for c in range(DC):
                sp.dma_start(ctx_raw[:, c, :], ctx_t[c]).then_inc(ctx_in[c], 16)
                if c >= 2:
                    sp.wait_ge(split_lo, 2 * (c - 1))
                sp.dma_start(wkv_raw[:, c % 2, :], wkv_t[c]).then_inc(wkv_in[c], 16)
                if c == DC - 1:
                    sp.dma_start(xres[:, :, :], x.rearrange("(r p) d -> p r d", p=P)).then_inc(x_in, 16)
                    sp.dma_start(gates[:, 0:1], g_xattn.to_broadcast([P, 1])).then_inc(g_in, 16)
                    sp.dma_start(gates[:, 1:2], g_ffn.to_broadcast([P, 1])).then_inc(g_in, 16)

            def load_wq(h):
                if h >= 2:
                    sp.wait_ge(wq_lo, h - 1)
                sp.dma_start(wq_raw[:, h % 2], wq_t[h].rearrange("p (c n) -> p c n", c=DC)).then_inc(wq_in[h % 2], 16)

            def load_codes(i):
                if i >= 2:
                    sp.wait_ge(line_step, i - 1)
                    sp.wait_ge(ramp_done, NR * (i - 1))
                sp.dma_start(code_in[:, i % 2, :], codes[i // 2, :, bass.ts(i % 2, HALF)]).then_inc(code_at[i % 2], 16)

            def load_scales(i):
                if i >= 2:
                    sp.wait_ge(w_stored[i % 2], 16 * (i // 2))
                for s in range(2):
                    sp.dma_start(scale_in[bass.ts(s, P // 2), i % 2, :],
                                 absmax[i // 2, s:s + 1, bass.ts(i % 2, HALF)].to_broadcast([P // 2, HALF])
                                 ).then_inc(scale_at[i % 2], 16)

            def store_chunk(i):
                sp.wait_ge(w_ready, i + 1)
                sp.dma_start(weights[i // 2, :, bass.ts(i % 2, HALF)], scale_in[:, i % 2, :]
                             ).then_inc(w_stored[i % 2], 16)

            def chunks_done(place):
                for n in SLOTS.get(place, []):
                    if n % STEPS == STEPS - 1:
                        i = n // STEPS
                        if i + 2 < CHUNKS:
                            load_codes(i + 2)
                        store_chunk(i)
                        if i + 2 < CHUNKS:
                            load_scales(i + 2)

            for i in range(2):
                load_codes(i)
                load_scales(i)
            load_wq(0)
            load_wq(1)
            for u in range(NU):
                chunks_done(("unit", u))
            for it in range(ITERS):
                if it % 4 == 0 and it // 4 + 2 < H:
                    load_wq(it // 4 + 2)
                if it % (RT * G) == 13 and it < TILES:
                    g = it // (RT * G)
                    if g == 0:
                        sp.wait_ge(unit_lo, NU)
                    else:
                        sp.wait_ge(misc_done, NM["wo", g - 1, RT - 1] + 1)
                    sp.dma_start(wo_raw[:, :, :], wo_t[g].rearrange("p (c n) -> p c n", c=OC)).then_inc(wo_in, 16)
                chunks_done(("att", it))

            for m in range(MT):
                chunks_done(("ffn", m))
            for r in range(RT):
                sp.wait_ge(res_done, r + 1)
                sp.dma_start(out[bass.ts(r, P), :], result[:, r, :]).then_inc(out_done, 16)
            sp.wait_ge(out_done, 16 * RT)

        @block.tensor
        def _(pe):
            def three(o, a, b, first, last):
                pe.matmul(o, a[0], b[0], start=first, stop=False)
                pe.matmul(o, a[0], b[1], start=False, stop=False)
                return pe.matmul(o, a[1], b[0], start=False, stop=last)

            def both(pair, *idx):
                return [t[idx] for t in pair]

            ALL = slice(None)
            for c in range(DC):
                pe.wait_ge(split_lo, 2 * (c + 1))
                for u, (_, t) in enumerate(V_CTX):
                    mm = three(bank[:, u, 0:KV * HD], both(ctxT, ALL, c, bass.ts(t, P)),
                               both(wkv, ALL, c, slice(KV * HD, 2 * KV * HD)), c == 0, c == DC - 1)
                    if c == DC - 1:
                        mm.then_inc(unit_done, 1)
            for u in range(len(V_CTX), NU):
                unit = UNITS[u]
                pe.wait_ge(unit_lo, u - 7)
                if unit[0] == "x":
                    if unit[1] == 0:
                        pe.wait_ge(xhat_done, RT)
                        pe.wait_ge(const_done, 1)
                    for r in range(RT):
                        mm = pe.transpose(bank[:, u % 8, bass.ts(r, P)], xhat[:, r, bass.ts(unit[1], P)], ident[:, :])
                    mm.then_inc(unit_done, 1)
                    continue
                if u == len(V_CTX + K_CTX + X_T):
                    pe.wait_ge(unit_lo, u)
                for c in range(DC):
                    if unit[0] == "v":
                        mm = three(bank[:, u % 8, 0:KV * HD], both(xT, ALL, c, bass.ts(unit[1] - 8, P)),
                                   both(wkv, ALL, c, slice(KV * HD, 2 * KV * HD)), c == 0, c == DC - 1)
                    else:
                        _, h, b = unit
                        rhs = both(ctxT, ALL, c, bass.ts(b, CTX)) if b < B else both(xT, ALL, c, ALL)
                        mm = three(bank[0:HD, u % 8, :], both(wkv, ALL, c, bass.ts(h, HD)), rhs, c == 0, c == DC - 1)
                mm.then_inc(unit_done, 1)

            def misc(n):
                _, kind, i, part = MISC[n]
                if n:
                    pe.wait_ge(misc_free, n)
                else:
                    pe.wait_ge(unit_lo, NU - 4)
                o = bank[:, 7, :]
                if kind == "q":
                    pe.wait_ge(wq_lo, i + 1)
                    for c in range(DC):
                        mm = three(bank[0:HD, 7, :], both(wq, ALL, i % 2, c, ALL), both(xT, ALL, c, ALL),
                                   c == 0, c == DC - 1)
                elif kind == "ot":
                    if part == 0:
                        pe.wait_ge(o_done, RT * G * (i + 1))
                    for r in range(RT):
                        mm = pe.transpose(bank[:, 7, bass.ts(r, P)], og[:, i % 2, r, bass.ts(part, P)], ident[:, :])
                else:
                    if part == 0:
                        pe.wait_ge(wo_lo, i + 1)
                    for c in range(OC):
                        mm = three(o, both(oT, ALL, c, bass.ts(part, P)), both(wo, ALL, c, ALL), c == 0, c == OC - 1)
                mm.then_inc(misc_done, 1)

            def scores(t):
                h, r = divmod(t, RT)
                b, kv = r // 2, h // G
                if r == 0:
                    pe.wait_ge(misc_free, NM["q", h, 0] + 1)
                if t == 0:
                    pe.wait_ge(unit_lo, NU)
                if t >= 2:
                    pe.wait_ge(exp_done, t - 1)
                s = 2 * (t % 2)
                for o, keys in ((bank[:, s, :], slice(0, 512)), (bank[:, s + 1, 0:KEYS - 512], slice(512, KEYS))):
                    mm = three(o, both(qT, ALL, h % 2, bass.ts(r, P)), both(kT, ALL, kv, b, keys), True, True)
                mm.then_inc(scores_done, 1)

            def transposes(t):
                pe.wait_ge(exp_done, t + 1)
                for k in range(2):
                    n = 2 * t + k
                    if n >= 2:
                        pe.wait_ge(pt_lo, n - 1)
                    for j in range(3):
                        mm = pe.transpose(bank[:, 4 + k, bass.ts(j, P)],
                                          prob[:, t % 3, bass.ts(3 * k + j, P)], ident[:, :])
                    mm.then_inc(tr_done, 1)

            def values(t):
                h, r = divmod(t, RT)
                b, kv = r // 2, h // G
                if t:
                    pe.wait_ge(o_done, t)
                o = bank[:, 6, 0:2 * HD]
                for j in range(KT):
                    if j % 3 == 0:
                        pe.wait_ge(pt_lo, 2 * t + j // 3 + 1)
                    rhs = v[:, b * KT + j, kv, :]
                    pe.matmul(o, probT[0][:, t % 2, bass.ts(j, P)], rhs, start=(j == 0), stop=False)
                    mm = pe.matmul(o, probT[1][:, t % 2, bass.ts(j, P)], rhs, start=False, stop=(j == KT - 1))
                mm.then_inc(pv_done, 1)

            misc(0)
            for it in range(ITERS):
                if it < TILES:
                    scores(it)
                if 0 <= it - TLAG < TILES:
                    transposes(it - TLAG)
                if 0 <= it - PLAG < TILES:
                    values(it - PLAG)
                for n, item in enumerate(MISC):
                    if item[0] == it:
                        misc(n)

            pe.wait_ge(o_done, TILES)
            pe.wait_ge(pt_lo, 2 * TILES)
            pe.wait_ge(misc_free, len(MISC))
            for c in range(OC):
                for r in range(RT):
                    mm = pe.transpose(bank[:, TAIL[c], bass.ts(r, P)], og[:, (KV - 1) % 2, r, bass.ts(c, P)],
                                      ident[:, :])
                mm.then_inc(tail_done, 1)
            pe.wait_ge(wo_lo, KV)
            for r in range(RT):
                for c in range(OC):
                    if r == 0:
                        pe.wait_ge(tail_lo, c + 1)
                    mm = three(bank[:, r, :], both(oT, ALL, c, bass.ts(r, P)), both(wo, ALL, c, ALL),
                               c == 0, c == OC - 1)
                mm.then_inc(rows_done, 1)

            for r in range(RT):
                pe.wait_ge(xhat_done, RT + r + 1)
                for c in range(DC):
                    mm = pe.transpose(bank[:, 4 + c, bass.ts(r, P)], xhat2[:, r, bass.ts(c, P)], ident[:, :])
            mm.then_inc(x2_done, 1)

            def down(m):
                pe.wait_ge(h_lo, m + 1)
                for r in range(RT):
                    mm = three(bank[:, r, :], both(hT, ALL, m % 2, bass.ts(r, P)),
                               both(wf, ALL, m % 3, slice(2 * D, FW)), m == 0, m == MT - 1)
                    if m == MT - 1:
                        mm.then_inc(y_done, 1)
                if m < MT - 1:
                    mm.then_inc(y_done, 1)

            for m in range(MT):
                pe.wait_ge(wf_lo, m + 1)
                if m >= 2:
                    pe.wait_ge(h_done, m - 1)
                for k, done in ((0, g_done), (1, u_done)):
                    for c in range(DC):
                        if m == 0:
                            pe.wait_ge(x2_lo, DC if k else c + 1)
                        mm = three(bank[:, 4 + 2 * (m % 2) + k, :], both(wf, ALL, m % 3, bass.ts(4 * k + c, P)),
                                   both(xT, ALL, c, ALL), c == 0, c == DC - 1)
                    mm.then_inc(done, 1)
                if m:
                    down(m - 1)
            down(MT - 1)

        @block.scalar
        def _(act):
            for c in range(DC):
                act.wait_ge(ctx_in[c], 16)
                act.copy(ctxT[0][:, c, :], ctx_raw[:, c, :]).then_inc(split_hi, 1)
                act.wait_ge(wkv_in[c], 16)
                act.copy(wkv[0][:, c, :], wkv_raw[:, c % 2, :]).then_inc(split_hi, 1)
            act.wait_ge(g_in, 32)
            act.activation(gate_tanh[:, :], gates[:, :], ACT.Tanh).then_inc(tanh_done, 1)

            def misc(n):
                _, kind, i, part = MISC[n]
                if kind == "wo":
                    return
                act.wait_ge(misc_done, n + 1)
                if kind == "q":
                    if n == 0:
                        act.wait_ge(unit_lo, NU)
                    act.mul(qT[0][:, i % 2, :], bank[0:HD, 7, :], SCALE).then_inc(misc_hi, 1)
                else:
                    act.copy(oT[0][:, part, :], bank[:, 7, :]).then_inc(misc_hi, 1)

            def ramp_steps(place):
                for k in MADE.get(place, []):
                    i, j = divmod(k, NR)
                    if j == 0:
                        act.wait_ge(code_at[i % 2], 16 * (i // 2 + 1))
                    if k >= RAMPS:
                        act.wait_ge(ramp_used, k - RAMPS + 1)
                    act.activation(ramp[:, k % RAMPS, :], code_in[:, i % 2, :], ACT.Relu,
                                   bias=ramp_bias[:, j:j + 1], scale=ramps[j][0]).then_inc(ramp_done, 1)

            act.wait_ge(zero_done, 1)
            for u, unit in enumerate(UNITS):
                src, hi, _ = unit_place(unit, u)
                act.wait_ge(unit_done, u + 1)
                act.copy(hi, src).then_inc(unit_hi, 1)
                ramp_steps(("unit", u))
            misc(0)
            for it in range(ITERS):
                if 0 <= it - TLAG < TILES:
                    t = it - TLAG
                    for k in range(2):
                        act.wait_ge(tr_done, 2 * t + k + 1)
                        if k == 0 and t >= 2:
                            act.wait_ge(pv_done, t - 1)
                        act.copy(probT[0][:, t % 2, bass.ts(k, 384)], bank[:, 4 + k, 0:384]).then_inc(pt_hi, 1)
                if 0 <= it - PLAG < TILES:
                    t = it - PLAG
                    act.wait_ge(pv_done, t + 1)
                    act.wait_ge(rinv_done, t + 1)
                    if t:
                        act.wait_ge(o_done, t)
                    act.mul(opart[:, :], bank[:, 6, HD:2 * HD], rinv[:, t:t + 1]).then_inc(o_part, 1)
                if it < TILES:
                    act.wait_ge(max_done, it + 1)
                    if it >= 3:
                        act.wait_ge(tr_done, 2 * (it - 2))
                    s = 2 * (it % 2)
                    act.activation(prob[:, it % 3, :], bank[:, s:s + 2, :].rearrange("p a n -> p (a n)")[:, 0:KEYS],
                                   ACT.Exp, bias=negmax[:, it % 4:it % 4 + 1],
                                   accum_out=rowsum[:, it:it + 1]).then_inc(exp_done, 1)
                for n, item in enumerate(MISC):
                    if item[0] == it:
                        misc(n)
                ramp_steps(("att", it))

            def load_wf(m):
                if m == 0:
                    act.wait_ge(scores_done, TILES)
                if m >= 2:
                    act.wait_ge(wf_lo, m - 1)
                for s in range(2):
                    act.wait_ge(w_stored[s], 16 * (m + 1))
                act.dma_start(wf_raw[:, m % 2, :], weights[m]).then_inc(wf_in[m % 2], 16)

            def split_wf(m):
                act.wait_ge(wf_in[m % 2], 16 * (m // 2 + 1))
                if m >= 3:
                    act.wait_ge(y_done, m - 2)
                act.copy(wf[0][:, m % 3, :], wf_raw[:, m % 2, :]).then_inc(wf_hi, 1)

            load_wf(0)
            load_wf(1)
            for c in range(OC):
                act.wait_ge(tail_done, c + 1)
                act.copy(oT[0][:, c, :], bank[:, TAIL[c], :]).then_inc(tail_hi, 1)
            split_wf(0)
            load_wf(2)
            act.wait_ge(x2_done, 1)
            for c in range(DC):
                act.copy(xT[0][:, c, :], bank[:, 4 + c, :]).then_inc(x2_hi, 1)
            for m in range(MT):
                if m + 1 < MT:
                    split_wf(m + 1)
                act.wait_ge(g_done, m + 1)
                if m >= 2:
                    act.wait_ge(h_done, m - 1)
                act.activation(sg[:, m % 2, :], bank[:, 4 + 2 * (m % 2), :], ACT.Silu, scale=-1.0).then_inc(sg_done, 1)
                ramp_steps(("ffn", m))
                if m + 3 < MT:
                    load_wf(m + 3)

        @block.vector
        def _(dve):
            ln_count = [0]

            def link(ins):
                ln_count[0] += 1
                ins.then_inc(ln_step, 1)
                dve.wait_ge(ln_step, ln_count[0])

            def layer_norm(dst, n, r):
                link(dve.bn_stats(stats[:, r, :], xres[:, r, :]))
                link(dve.bn_aggr(meanvar[:, r, :], stats[:, r, :]))
                dve.tensor_scalar(vareps[:, r:r + 1], meanvar[:, r, 1:2], EPS, None, ALU.add).then_inc(var_done, 1)
                dve.wait_ge(rough_done, n * RT + r + 1)
                rr = rough[:, r:r + 1]
                link(dve.tensor_tensor(newton[:, 0, r:r + 1], rr, rr, ALU.mult))
                link(dve.scalar_tensor_tensor(out=newton[:, 1, r:r + 1], in0=newton[:, 0, r:r + 1], scalar=-0.5,
                                              in1=vareps[:, r:r + 1], op0=ALU.mult, op1=ALU.mult))
                link(dve.scalar_tensor_tensor(out=rstd[:, r:r + 1], in0=newton[:, 1, r:r + 1], scalar=1.5, in1=rr,
                                              op0=ALU.add, op1=ALU.mult))
                dve.tensor_scalar(dst[:, r, :], xres[:, r, :], meanvar[:, r, 0:1], rstd[:, r:r + 1],
                                  ALU.subtract, ALU.mult).then_inc(xhat_done, 1)

            for j, (_, b, _) in enumerate(ramps):
                ins = dve.memset(ramp_bias[:, j:j + 1], b)
            dve.memset(neghalf[:, :], -0.5).then_inc(zero_done, 1)
            for c in range(DC):
                dve.wait_ge(split_hi, 2 * c + 1)
                dve.tensor_tensor(ctxT[1][:, c, :], ctx_raw[:, c, :], f32(ctxT[0][:, c, :]),
                                  ALU.subtract).then_inc(split_lo, 1)
                dve.wait_ge(split_hi, 2 * c + 2)
                dve.tensor_tensor(wkv[1][:, c, :], wkv_raw[:, c % 2, :], f32(wkv[0][:, c, :]),
                                  ALU.subtract).then_inc(split_lo, 1)

            def split_wq(h):
                dve.wait_ge(wq_in[h % 2], 16 * (h // 2 + 1))
                if h >= 2:
                    dve.wait_ge(misc_done, NM["q", h - 2, 0] + 1)
                dve.tensor_copy(wq[0][:, h % 2], wq_raw[:, h % 2]).then_inc(wq_hi, 1)

            def dequant_steps(place):
                for k in SLOTS.get(place, []):
                    i, j = divmod(k, NR)
                    dve.wait_ge(ramp_done, k + 1)
                    if j == 0:
                        dve.wait_ge(line_step, i + 1)
                    else:
                        dve.wait_ge(ramp_used, k)
                    dve.scalar_tensor_tensor(out=acc[:, i % 2, :], in0=ramp[:, k % RAMPS, :], scalar=ramps[j][2],
                                             in1=acc[:, i % 2, :], op0=ALU.min, op1=ALU.add).then_inc(ramp_used, 1)

            for u, unit in enumerate(UNITS):
                if u == 8:
                    dve.wait_ge(x_in, 16)
                    for r in range(RT):
                        layer_norm(xhat, 0, r)
                    split_wq(0)
                    split_wq(1)
                src, hi, lo = unit_place(unit, u)
                dve.wait_ge(unit_hi, u + 1)
                dve.tensor_tensor(lo, src, f32(hi), ALU.subtract).then_inc(unit_lo, 1)
                dequant_steps(("unit", u))

            def misc(n):
                _, kind, i, part = MISC[n]
                if kind == "wo":
                    if (i, part) == (0, 0):
                        dve.wait_ge(tanh_done, 1)
                    dve.wait_ge(misc_done, n + 1)
                    dve.scalar_tensor_tensor(out=xres[:, part, :], in0=bank[:, 7, :], scalar=gate_tanh[:, 0:1],
                                             in1=xres[:, part, :], op0=ALU.mult, op1=ALU.add).then_inc(misc_free, 1)
                    return
                dve.wait_ge(misc_hi, Q_HI[n] + 1)
                if kind == "q":
                    dve.scalar_tensor_tensor(out=qT[1][:, i % 2, :], in0=bank[0:HD, 7, :], scalar=SCALE,
                                             in1=f32(qT[0][:, i % 2, :]), op0=ALU.mult,
                                             op1=ALU.subtract).then_inc(misc_free, 1)
                else:
                    dve.tensor_tensor(oT[1][:, part, :], bank[:, 7, :], f32(oT[0][:, part, :]),
                                      ALU.subtract).then_inc(misc_free, 1)

            misc(0)
            for it in range(ITERS):
                if it < TILES:
                    s = 2 * (it % 2)
                    dve.wait_ge(scores_done, it + 1)
                    if it >= 4:
                        dve.wait_ge(exp_done, it - 3)
                    dve.tensor_reduce(negmax[:, it % 4:it % 4 + 1],
                                      bank[:, s:s + 2, :].rearrange("p a n -> p (a n)")[:, 0:KEYS],
                                      AX.X, ALU.max, negate=True).then_inc(max_done, 1)
                if 0 <= it - TLAG < TILES:
                    t = it - TLAG
                    for k in range(2):
                        dve.wait_ge(pt_hi, 2 * t + k + 1)
                        dve.tensor_tensor(probT[1][:, t % 2, bass.ts(k, 384)], bank[:, 4 + k, 0:384],
                                          f32(probT[0][:, t % 2, bass.ts(k, 384)]), ALU.subtract).then_inc(pt_lo, 1)
                    dve.wait_ge(exp_done, t + 1)
                    dve.reciprocal(rinv[:, t:t + 1], rowsum[:, t:t + 1]).then_inc(rinv_done, 1)
                if 0 <= it - PLAG < TILES:
                    t = it - PLAG
                    h, r = divmod(t, RT)
                    g = h // G
                    dve.wait_ge(o_part, t + 1)
                    if r == 0 and h % G == 0 and g >= 2:
                        dve.wait_ge(misc_done, NM["ot", g - 2, OC - 1] + 1)
                    dve.wait_ge(rinv_done, t + 1)
                    dve.scalar_tensor_tensor(out=og[:, g % 2, r, bass.ts(h % G, HD)], in0=bank[:, 6, 0:HD],
                                             scalar=rinv[:, t:t + 1], in1=opart[:, :], op0=ALU.mult,
                                             op1=ALU.add).then_inc(o_done, 1)
                for n, item in enumerate(MISC):
                    if item[0] == it:
                        misc(n)
                if it % 4 == 2 and it // 4 + 2 < H:
                    split_wq(it // 4 + 2)
                if it >= RT * G and it % (RT * G) == 2:
                    dve.wait_ge(wo_in, it // (RT * G) * 16)
                    dve.tensor_copy(wo[0][:, :, :], wo_raw[:, :, :]).then_inc(wo_hi, 1)
                dequant_steps(("att", it))

            for c in range(OC):
                dve.wait_ge(tail_hi, c + 1)
                dve.tensor_tensor(oT[1][:, c, :], bank[:, TAIL[c], :], f32(oT[0][:, c, :]),
                                  ALU.subtract).then_inc(tail_lo, 1)
            for r in range(RT):
                dve.wait_ge(rows_done, r + 1)
                link(dve.scalar_tensor_tensor(out=xres[:, r, :], in0=bank[:, r, :], scalar=gate_tanh[:, 0:1],
                                              in1=xres[:, r, :], op0=ALU.mult, op1=ALU.add))
                layer_norm(xhat2, 1, r)
            for c in range(DC):
                dve.wait_ge(x2_hi, c + 1)
                dve.tensor_tensor(xT[1][:, c, :], bank[:, 4 + c, :], f32(xT[0][:, c, :]),
                                  ALU.subtract).then_inc(x2_lo, 1)
            for m in range(MT):
                dve.wait_ge(u_done, m + 1)
                dve.wait_ge(sg_done, m + 1)
                dve.tensor_tensor(hid[:, m % 2, :], bank[:, 5 + 2 * (m % 2), :], sg[:, m % 2, :],
                                  ALU.mult).then_inc(h_done, 1)
                dve.wait_ge(h_done, m + 1)
                if m >= 2:
                    dve.wait_ge(y_done, m - 1)
                dve.tensor_copy(hT[0][:, m % 2, :], hid[:, m % 2, :]).then_inc(h_hi, 1)
                dve.wait_ge(h_hi, m + 1)
                dve.tensor_tensor(hT[1][:, m % 2, :], hid[:, m % 2, :], f32(hT[0][:, m % 2, :]),
                                  ALU.subtract).then_inc(h_lo, 1)
                dequant_steps(("ffn", m))
            for r in range(RT):
                dve.wait_ge(y_done, MT + r)
                dve.scalar_tensor_tensor(out=result[:, r, :], in0=bank[:, r, :], scalar=gate_tanh[:, 1:2],
                                         in1=xres[:, r, :], op0=ALU.mult, op1=ALU.add).then_inc(res_done, 1)

        @block.gpsimd
        def _(pool):
            pool.memset(ident[:, :], 0.0).then_inc(zero_done, 1)
            pool.wait_ge(zero_done, 2)
            pool.affine_select(out=ident[:, :], in_=ident[:, :], compare_op=ALU.not_equal, fill=1.0, base=0,
                               pattern=[[-1, P]], channel_multiplier=1).then_inc(const_done, 1)

            def rough_power(n, r):
                pool.wait_ge(var_done, n * RT + r + 1)
                pool.tensor_tensor(rough[:, r:r + 1], vareps[:, r:r + 1], neghalf[:, 0:1], ALU.pow
                                   ).then_inc(rough_done, 1)

            def line(i):
                pool.wait_ge(code_at[i % 2], 16 * (i // 2 + 1))
                if i >= 2:
                    pool.wait_ge(w_ready, i - 1)
                pool.tensor_scalar(acc[:, i % 2, :], code_in[:, i % 2, :], -slope, offset, ALU.mult,
                                   ALU.add).then_inc(line_step, 1)

            def multiply(place):
                for k in SLOTS.get(place, []):
                    i, j = divmod(k, NR)
                    if j == 0 and i + 1 < CHUNKS:
                        line(i + 1)
                    if j == STEPS - 1:
                        pool.wait_ge(scale_at[i % 2], 32 * (i // 2 + 1))
                        pool.wait_ge(ramp_used, NR * (i + 1))
                        pool.tensor_tensor(scale_in[:, i % 2, :], acc[:, i % 2, :], scale_in[:, i % 2, :],
                                           ALU.mult).then_inc(w_ready, 1)

            def split_wq(h):
                pool.wait_ge(wq_hi, h + 1)
                pool.tensor_tensor(wq[1][:, h % 2], wq_raw[:, h % 2], f32(wq[0][:, h % 2]),
                                   ALU.subtract).then_inc(wq_lo, 1)

            for r in range(RT):
                rough_power(0, r)
            split_wq(0)
            split_wq(1)
            line(0)
            for u in range(NU):
                multiply(("unit", u))
            for it in range(ITERS):
                if it % 4 == 2 and it // 4 + 2 < H:
                    split_wq(it // 4 + 2)
                if it >= RT * G and it % (RT * G) == 2:
                    pool.wait_ge(wo_hi, it // (RT * G))
                    pool.tensor_tensor(wo[1][:, :, :], wo_raw[:, :, :], f32(wo[0][:, :, :]),
                                       ALU.subtract).then_inc(wo_lo, 1)
                multiply(("att", it))

            for r in range(RT):
                rough_power(1, r)
            def split_wf(m):
                pool.wait_ge(wf_hi, m + 1)
                pool.tensor_tensor(wf[1][:, m % 3, :], wf_raw[:, m % 2, :], f32(wf[0][:, m % 3, :]),
                                   ALU.subtract).then_inc(wf_lo, 1)

            split_wf(0)
            for m in range(MT):
                if m + 1 < MT:
                    split_wf(m + 1)
                multiply(("ffn", m))


def kernel(**inputs):
    import numpy as np
    import concourse.bacc as bacc
    from concourse.bass_utils import run_bass_kernel_spmd

    a = {k: np.asarray(x) for k, x in inputs.items()}

    def tiles_of(w):
        return w.T.reshape(DC, P, MT, P).transpose(2, 1, 0, 3).reshape(MT, P, DC * P)

    def scales_of(s):
        return s.reshape(MT, P, DC, 2).transpose(0, 3, 2, 1).reshape(MT, 2, DC * P)

    arrays = {
        "x": a["x"].reshape(ROWS, D),
        "ctx_t": a["ctx_4096"].reshape(B * CTX, D).T.reshape(DC, P, B * CTX),
        "wkv_t": np.concatenate([a["L0_xattn_Wk"].T, a["L0_xattn_Wv"].T], axis=1).reshape(DC, P, 2 * KV * HD),
        "wq_t": a["L0_xattn_Wq"].T.reshape(DC, P, H, HD).transpose(2, 1, 0, 3).reshape(H, P, DC * HD),
        "wo_t": a["L0_xattn_Wo"].T.reshape(KV, OC, P, D).transpose(0, 2, 1, 3).reshape(KV, P, OC * D),
        "codes": np.concatenate([
            tiles_of(a["L0_ffn_gate_q"]), tiles_of(a["L0_ffn_up_q"]),
            a["L0_ffn_down_q"].T.reshape(MT, P, D)], axis=2),
        "absmax": np.concatenate([
            scales_of(a["L0_ffn_gate_absmax"]), scales_of(a["L0_ffn_up_absmax"]),
            a["L0_ffn_down_absmax"].reshape(D, MT, 2).transpose(1, 2, 0)], axis=2),
        "g_xattn": a["g_xattn"].reshape(1, 1),
        "g_ffn": a["g_ffn"].reshape(1, 1),
    }
    nc = bacc.Bacc("TRN2", target_bir_lowering=False, num_devices=1, dynamic_dma_scratch_size=1024)
    arrays = {k: np.ascontiguousarray(x) for k, x in arrays.items()}
    args = [nc.dram_tensor(f"in_{k}", x.shape, mybir.dt.from_np(x.dtype), kind="ExternalInput").ap()
            for k, x in arrays.items()]
    weights = nc.dram_tensor("ffn_weights", (MT, P, FW), F32, kind="Internal").ap()
    out = nc.dram_tensor("out", (ROWS, D), F32, kind="ExternalOutput").ap()
    flamingo_block(nc, *args, weights, out)
    r = run_bass_kernel_spmd(nc, [{f"in_{k}": x for k, x in arrays.items()}], core_ids=[0])
    return r.results[0]["out"].reshape(B, SEQ, D)
```

```python
from contextlib import ExitStack

import concourse.bass as bass
from concourse import mybir

P = 128
ROWS, D = 512, 512
RT, DC = ROWS // P, D // P
B, CTX, SEQ = 2, 512, 256
KEYS = CTX + SEQ
KT = KEYS // P
H, KV, HD = 16, 4, 96
G = H // KV
M = 1792
MT = M // P
SCALE = float(HD) ** -0.5
EPS = 1e-5
TILES = H * RT
FW = 3 * D
HALF = FW // 2
CHUNKS = 2 * MT
OC = G * HD // P

F32 = mybir.dt.float32
F32R = mybir.dt.float32r
I32 = mybir.dt.int32
ALU = mybir.AluOpType
ACT = mybir.ActivationFunctionType
AX = mybir.AxisListType

NF4 = [-1.0, -0.6961928009986877, -0.5250730514526367, -0.39491748809814453, -0.28444138169288635,
       -0.18477343022823334, -0.09105003625154495, 0.0, 0.07958029955625534, 0.16093020141124725,
       0.24611230194568634, 0.33791524171829224, 0.44070982933044434, 0.5626170039176941,
       0.7229568362236023, 1.0]


def nf4_ramps():
    step = [NF4[i + 1] - NF4[i] for i in range(15)]
    slope = step[0]
    rest = [slope - s for s in step]
    ramps = []
    for left, full, right in ((1, 13, 14), (2, 3, 12), (4, 5, 11), (6, 9, 10), (7, 8, 9)):
        if (left, full) == (7, 8):
            left, full = None, 7
            right = 8
        w, z = rest[full], rest[right]
        x = rest[left] if left is not None else 0.0
        first = left + 1 if left is not None else full
        ramps.append((w, x - w * first, x + (right - first) * w + z))
        if left is not None:
            rest[left] = 0.0
        for i in range(first, right):
            rest[i] -= w
        rest[right] = 0.0
    return slope, -NF4[0], ramps


def tile_at(t):
    g, t = divmod(t, RT * G)
    b, t = divmod(t, RT // B * G)
    j, r = divmod(t, RT // B)
    return g * G + j, RT // B * b + r


def misc_items():
    items = [(Q_AT[h], "q", h, 0) for h in range(H)]
    items += [(GT * g + at, "wo", g, r) for g in range(KV - 1) for r, at in enumerate((13, 17, 21, 23))]
    last = GT * (KV - 1)
    items += [(last + at, kind, r, 0) for kind, r, at in (
        ("rw", 0, 13), ("rw", 1, 15), ("x2", 0, 16), ("x2", 1, 17), ("rw", 2, 20), ("rw", 3, 20), ("x2", 2, 20),
        ("x2", 3, 20))]
    return sorted(items, key=lambda item: item[0])


RAMPS = 2
DEEP = 6
GT = RT * G
TLAG, PLAG = 3, 4
ITERS = TILES + PLAG
Q_AT = [-1, -1, 2, 4] + [GT * g + at for g in range(1, KV) for at in (-5, -1, 2, 3)]
WQ_AT = [-1, -1, 0, 1] + [GT * g + at for g in range(1, KV) for at in (-8, -4, -2, 0)]
WQ_SPLIT = {WQ_AT[h]: h for h in range(2, H)}
WQ_LOAD = {WQ_AT[h - 2]: h for h in range(4, H)}
WO_LOAD = {5: 0, **{GT * g + 7: g for g in range(1, KV)}}
WO_SPLIT = {GT * g + 9 + c: (g, c) for g in range(KV) for c in range(OC)}
STEPS = [(i, j) for i in range(CHUNKS) for j in range(5)]
STEPS_TO = [sum(i < n for i, _ in STEPS) for n in range(CHUNKS + 1)]
LEAD = 1
UNIT_STEPS = [0] * 8 + [1] * 3 + [0] * 4 + [1] * 10


def dequant_slots(units):
    slots, n = {}, 0
    places = [(("unit", u), UNIT_STEPS[u]) for u in range(units)]
    heavy = {it for it, kind, _, _ in misc_items() if kind == "q"}
    places += [(("att", it), 2 if it in heavy else 1) for it in range(TILES)]
    places += [(("ffn", m), 5 if m else 2) for m in range(MT)]
    for place, k in places:
        slots[place] = list(range(n, min(n + k, len(STEPS))))
        n += len(slots[place])
    assert n == len(STEPS)
    made, k = {}, 0
    for place, _ in places:
        made[place] = list(range(k, min(max(slots[place], default=k - 1 - LEAD) + LEAD + 1, n)))
        k += len(made[place])
    return slots, made


def flamingo_block(nc, x, ctx_t, wkv_t, wq_t, wo_t, codes, absmax, g_xattn, g_ffn, weights, out):
    slope, offset, ramps = nf4_ramps()
    NR = len(ramps)
    MISC = misc_items()
    NM = {(k, i, p): n for n, (_, k, i, p) in enumerate(MISC)}
    Q_HI = {}
    n_hi = 0
    for n, (_, k, i, p) in enumerate(MISC):
        Q_HI[n] = n_hi
        n_hi += k not in ("wo", "rw")

    with ExitStack() as ctx:
        def sem(name):
            return ctx.enter_context(nc.semaphore(name))

        fixed, att_kv, early, att, ffn = (ExitStack() for _ in range(5))

        def sb(stack, name, shape, dt):
            return stack.enter_context(nc.sbuf_tensor(name, shape, dt))

        bank = ctx.enter_context(nc.psum_tensor("bank", [P, 8, 512], F32))

        xres = sb(fixed, "xres", [P, RT, D], F32)
        xT = [sb(fixed, f"xT_{s}", [P, DC, ROWS], F32R) for s in ("hi", "lo")]
        ident = sb(fixed, "ident", [P, P], F32)
        stats = sb(fixed, "stats", [P, RT, 6], F32)
        meanvar = sb(fixed, "meanvar", [P, RT, 2], F32)
        vareps = sb(fixed, "vareps", [P, RT], F32)
        neghalf = sb(fixed, "neghalf", [P, RT], F32)
        rough = sb(fixed, "rough", [P, RT], F32)
        newton = sb(fixed, "newton", [P, 2, RT], F32)
        rstd = sb(fixed, "rstd", [P, RT], F32)
        gates = sb(fixed, "gates", [P, 2], F32)
        gate_tanh = sb(fixed, "gate_tanh", [P, 2], F32)
        ramp_bias = sb(fixed, "ramp_bias", [P, NR], F32)
        negmax = sb(fixed, "negmax", [P, 4], F32)
        rowsum = sb(fixed, "rowsum", [P, TILES], F32)
        rinv = sb(fixed, "rinv", [P, TILES], F32)
        wq_raw = sb(fixed, "wq_raw", [P, 2, DC, HD], F32)
        wq = [sb(fixed, f"wq_{s}", [P, 2, DC, HD], F32R) for s in ("hi", "lo")]
        code_in = sb(fixed, "code_in", [P, 2, HALF], I32)
        scale_in = sb(fixed, "scale_in", [P, 2, HALF], F32)
        acc = sb(fixed, "acc", [P, 2, HALF], F32)
        ramp = sb(fixed, "ramp", [P, RAMPS, HALF], F32)
        kT = [sb(att_kv, f"kT_{s}", [HD, KV, B, KEYS], F32R) for s in ("hi", "lo")]
        v = sb(att_kv, "v", [P, B * KT, KV, 2 * HD], F32R)
        raw = ExitStack()
        ctx_raw = sb(raw, "ctx_raw", [P, DC, B * CTX], F32)
        raw.close()
        xhat = sb(early, "xhat", [P, 2 * RT, D], F32)
        wkv_raw = sb(early, "wkv_raw", [P, 2, 2 * KV * HD], F32)
        ctxT = [sb(early, f"ctxT_{s}", [P, DC, B * CTX], F32R) for s in ("hi", "lo")]
        wkv = [sb(early, f"wkv_{s}", [P, DC, 2 * KV * HD], F32R) for s in ("hi", "lo")]
        early.close()
        qT = [sb(att, f"qT_{s}", [HD, G, ROWS], F32R) for s in ("hi", "lo")]
        prob = sb(att, "prob", [P, 3, KEYS], F32)
        probT = [sb(att, f"probT_{s}", [P, 2, KT, 2 * P], F32R) for s in ("hi", "lo")]
        oT = [sb(att, f"oT_{s}", [P, OC, ROWS], F32R) for s in ("hi", "lo")]
        raw = ExitStack()
        wo_raw = sb(raw, "wo_raw", [P, OC, D], F32)
        raw.close()
        wo_lo_part = sb(att, "wo_lo", [P, OC, D], F32R)
        wo = [sb(att, "wo_hi", [P, OC, D], F32R), wo_lo_part]
        xhat2 = sb(att, "xhat2", [P, 2, D], F32)
        att.close()
        att_kv.close()
        wf_raw = sb(ffn, "wf_raw", [P, 2, FW], F32)
        wf = [sb(ffn, f"wf_{s}", [P, 3, FW], F32R) for s in ("hi", "lo")]
        sg = sb(ffn, "sg", [P, 2, ROWS], F32)
        hid = sb(ffn, "hid", [P, 2, ROWS], F32)
        hT = [sb(ffn, f"hT_{s}", [P, 2, ROWS], F32R) for s in ("hi", "lo")]
        ramp_deep = sb(ffn, "ramp_deep", [P, DEEP, HALF], F32)
        result = sb(ffn, "result", [P, RT, D], F32)
        ffn.close()
        fixed.close()

        x_in, g_in, wo_in = sem("x_in"), sem("g_in"), sem("wo_in")
        ctx_in, wkv_in = [[sem(f"{n}_in{i}") for i in range(k * DC)] for n, k in (("ctx", B), ("wkv", 1))]
        wq_in, code_at, scale_at, w_stored, wf_in = [
            [sem(f"{n}{i}") for i in range(2)] for n in ("wq_in", "code_at", "scale_at", "w_stored", "wf_in")]
        out_done = sem("out_done")
        const_done, zero_done = sem("const_done"), sem("zero_done")
        tanh_done = sem("tanh_done")
        ln_step, var_done, rough_done, xhat_done = sem("ln_step"), sem("var_done"), sem("rough_done"), sem("xhat_done")
        split_hi, split_lo = sem("split_hi"), sem("split_lo")
        unit_done, unit_hi, unit_lo = sem("unit_done"), sem("unit_hi"), sem("unit_lo")
        wq_hi, wq_lo, wo_hi, wo_lo = sem("wq_hi"), sem("wq_lo"), sem("wo_hi"), sem("wo_lo")
        scores_done, max_done, exp_done = sem("scores_done"), sem("max_done"), sem("exp_done")
        tr_done, pt_hi, pt_lo = sem("tr_done"), sem("pt_hi"), sem("pt_lo")
        rinv_done, norm_done = sem("rinv_done"), sem("norm_done")
        pv_done, o_hi, o_lo = sem("pv_done"), sem("o_hi"), sem("o_lo")
        misc_done, misc_hi, misc_free = sem("misc_done"), sem("misc_hi"), sem("misc_free")
        line_step, ramp_done, ramp_used, w_ready = (
            sem("line_step"), sem("ramp_done"), sem("ramp_used"), sem("w_ready"))
        wf_hi, wf_lo = sem("wf_hi"), sem("wf_lo")
        g_done, u_done, y_done = sem("g_done"), sem("u_done"), sem("y_done")
        sg_done, h_done, h_hi, h_lo, res_done = (
            sem("sg_done"), sem("h_done"), sem("h_hi"), sem("h_lo"), sem("res_done"))

        block = ctx.enter_context(nc.Block())

        V_CTX = [("v", t) for t in range(B * CTX // P)]
        K_CTX = [("k", j, b) for b in range(B) for j in range(OC)]
        X_T = [("x", c) for c in range(DC)]
        V_X = [("v", B * CTX // P + r) for r in range(RT)]
        K_X = [("k", j, B) for j in range(OC)]
        UNITS = V_CTX + K_CTX[:OC] + X_T + K_CTX[OC:] + V_X + K_X
        NU = len(UNITS)
        U_Q = {NU - 6: 0, NU - 4: 1}
        SLOTS, MADE = dequant_slots(NU)

        def unit_bank(u):
            return u if u < 8 else (u - 8) % 7

        def unit_places(unit, u):
            o = bank[:, unit_bank(u), :]
            if unit[0] == "v":
                t = unit[1]
                tile = (t // 4) * KT + t % 4 if t < 8 else ((t - 8) // 2) * KT + 4 + t % 2
                return [(o[:, 0:KV * HD].rearrange("p (h d) -> p h d", h=KV), v[:, tile, :, 0:HD],
                         v[:, tile, :, HD:2 * HD])]
            if unit[0] == "x":
                return [(o, xT[0][:, unit[1], :], xT[1][:, unit[1], :])]
            _, j, b = unit
            pieces = []
            for h, rows, at in ((j, slice(0, HD), slice(0, HD)), (OC, slice(HD, P), bass.ts(j, P - HD))):
                src = bank[rows, unit_bank(u), :]
                if b < B:
                    pieces.append((src, kT[0][at, h, b, 0:CTX], kT[1][at, h, b, 0:CTX]))
                else:
                    pieces.append((src.rearrange("p (b s) -> p b s", b=B), kT[0][at, h, :, CTX:KEYS],
                                   kT[1][at, h, :, CTX:KEYS]))
            return pieces

        deep = SLOTS["ffn", 1][0] + LEAD

        def ramp_at(k):
            return ramp[:, k % RAMPS, :] if k < deep else ramp_deep[:, (k - deep) % DEEP, :]

        def row_place(r):
            return [t[:, :, bass.ts(r, P)] for t in xT], bank[:, 7, 0:DC * P].rearrange("p (c n) -> p c n", c=DC)

        def pair_places(p):
            h, r = tile_at(2 * p)
            j, cols = h % G, slice(r * P, (r + 2) * P)
            if j < OC:
                return [(oT[0][0:HD, j, cols], oT[1][0:HD, j, cols], bank[0:HD, 6, 0:2 * P])]
            return [(oT[0][HD:P, c, cols], oT[1][HD:P, c, cols], bank[bass.ts(c, P - HD), 6, 0:2 * P])
                    for c in range(OC)]

        def pieces_before(p):
            return (G - 1 + OC) * (p // G) + p % G

        def prob_place(t, k):
            return ([q[:, t // 2 % 2, 3 * k:3 * k + 3, bass.ts(t % 2, P)] for q in probT],
                    bank[:, 4 + k, 0:3 * P].rearrange("p (c n) -> p c n", c=3))

        def chunk_parts(c):
            cols = (slice(KV * HD, 2 * KV * HD), slice(0, KV * HD))
            ctx_part = [([t[:, c, bass.ts(b, CTX)] for t in ctxT], ctx_raw[:, c, bass.ts(b, CTX)],
                         (ctx_in[B * c + b], 16)) for b in range(B)]
            w_part = [([t[:, c, s] for t in wkv], wkv_raw[:, c % 2, s], (wkv_in[c], 16)) for s in cols]
            return [w_part[0], *ctx_part, w_part[1]]

        def f32(ap):
            return ap.bitcast(F32)

        @block.sync
        def _(sp):
            for c in range(DC):
                if c == DC - 1:
                    sp.dma_start(xres[:, :, :], x.rearrange("(r p) d -> p r d", p=P)).then_inc(x_in, 16)
                if c >= 2:
                    sp.wait_ge(split_lo, 4 * (c - 1))
                sp.dma_start(wkv_raw[:, c % 2, :], wkv_t[c]).then_inc(wkv_in[c], 16)
                for b in range(B):
                    sp.dma_start(ctx_raw[:, c, bass.ts(b, CTX)], ctx_t[c, :, bass.ts(b, CTX)]
                                 ).then_inc(ctx_in[B * c + b], 16)
            sp.dma_start(gates[:, 0:1], g_xattn.to_broadcast([P, 1])).then_inc(g_in, 16)
            sp.dma_start(gates[:, 1:2], g_ffn.to_broadcast([P, 1])).then_inc(g_in, 16)

            def load_wq(h):
                if h >= 2:
                    sp.wait_ge(wq_lo, h - 1)
                sp.dma_start(wq_raw[:, h % 2], wq_t[h].rearrange("p (c n) -> p c n", c=DC)).then_inc(wq_in[h % 2], 16)

            def load_codes(i):
                if i >= 2:
                    sp.wait_ge(line_step, i - 1)
                    sp.wait_ge(ramp_done, STEPS_TO[i - 1])
                sp.dma_start(code_in[:, i % 2, :], codes[i // 2, :, bass.ts(i % 2, HALF)]).then_inc(code_at[i % 2], 16)

            def load_scales(i):
                if i >= 2:
                    sp.wait_ge(w_stored[i % 2], 16 * (i // 2))
                for s in range(2):
                    sp.dma_start(scale_in[bass.ts(s, P // 2), i % 2, :],
                                 absmax[i // 2, s:s + 1, bass.ts(i % 2, HALF)].to_broadcast([P // 2, HALF])
                                 ).then_inc(scale_at[i % 2], 16)

            def store_chunk(i):
                sp.wait_ge(w_ready, i + 1)
                sp.dma_start(weights[i // 2, :, bass.ts(i % 2, HALF)], scale_in[:, i % 2, :]
                             ).then_inc(w_stored[i % 2], 16)

            def chunks_done(place):
                for n in SLOTS.get(place, []):
                    i, _ = STEPS[n]
                    if n + 1 == STEPS_TO[i + 1]:
                        if i + 2 < CHUNKS:
                            load_codes(i + 2)
                        store_chunk(i)
                        if i + 2 < CHUNKS:
                            load_scales(i + 2)

            for i in range(2):
                load_codes(i)
                load_scales(i)
            load_wq(0)
            load_wq(1)
            load_wq(2)
            load_wq(3)
            for u in range(NU):
                chunks_done(("unit", u))
            for it in range(ITERS):
                if it in WQ_LOAD:
                    load_wq(WQ_LOAD[it])
                if it in WO_LOAD:
                    g = WO_LOAD[it]
                    if g == 0:
                        sp.wait_ge(unit_lo, NU)
                    else:
                        sp.wait_ge(misc_done, NM["wo", g - 1, RT - 1] + 1)
                    sp.dma_start(wo_raw[:, :, :], wo_t[g].rearrange("p (c n) -> p c n", c=OC)).then_inc(wo_in, 16)
                chunks_done(("att", it))

            for m in range(MT):
                chunks_done(("ffn", m))
            for r in range(RT):
                sp.wait_ge(res_done, r + 1)
                sp.dma_start(out[bass.ts(r, P), :], result[:, r, :]).then_inc(out_done, 16)
            sp.wait_ge(out_done, 16 * RT)

        @block.tensor
        def _(pe):
            def three(o, a, b, first, last):
                pe.matmul(o, a[0], b[0], start=first, stop=False)
                pe.matmul(o, a[0], b[1], start=False, stop=False)
                return pe.matmul(o, a[1], b[0], start=False, stop=last)

            def both(pair, *idx):
                return [t[idx] for t in pair]

            ALL = slice(None)
            for c in range(DC):
                for u, (_, t) in enumerate(V_CTX):
                    if u % 4 == 0:
                        pe.wait_ge(split_lo, 4 * c + 2 + u // 4)
                    mm = three(bank[:, u, 0:KV * HD], both(ctxT, ALL, c, bass.ts(t, P)),
                               both(wkv, ALL, c, slice(KV * HD, 2 * KV * HD)), c == 0, c == DC - 1)
                    if c == DC - 1:
                        mm.then_inc(unit_done, 1)

            def misc(n):
                _, kind, i, part = MISC[n]
                if n:
                    pe.wait_ge(misc_free, n)
                else:
                    pe.wait_ge(unit_lo, UNITS.index(X_T[-1]) + 1)
                o = bank[:, 7, :]
                if kind == "q":
                    pe.wait_ge(wq_lo, i + 1)
                    for c in range(DC):
                        mm = three(bank[0:HD, 7, :], both(wq, ALL, i % 2, c, ALL), both(xT, ALL, c, ALL),
                                   c == 0, c == DC - 1)
                elif kind == "x2":
                    pe.wait_ge(xhat_done, RT + i + 1)
                    for c in range(DC):
                        mm = pe.transpose(bank[:, 7, bass.ts(c, P)], xhat2[:, i % 2, bass.ts(c, P)], ident[:, :])
                else:
                    g, r = (i, part) if kind == "wo" else (KV - 1, i)
                    if r == 0:
                        pe.wait_ge(wo_lo, OC * (g + 1))
                    done = pieces_before((GT * g + GT // B * (r // 2 + 1)) // 2)
                    for c in range(OC):
                        pe.wait_ge(o_lo, done - (OC - 1 - c))
                        mm = three(o, both(oT, ALL, c, bass.ts(r, P)), both(wo, ALL, c, ALL), c == 0, c == OC - 1)
                mm.then_inc(misc_done, 1)

            pe.wait_ge(split_lo, 4 * DC)
            for u in range(len(V_CTX), NU):
                unit = UNITS[u]
                pe.wait_ge(unit_lo, u - 7 if u < 15 else u - 6)
                if unit[0] == "x":
                    if unit[1] == 0:
                        pe.wait_ge(xhat_done, RT)
                        pe.wait_ge(const_done, 1)
                    for r in range(RT):
                        mm = pe.transpose(bank[:, unit_bank(u), bass.ts(r, P)], xhat[:, r, bass.ts(unit[1], P)], ident[:, :])
                    mm.then_inc(unit_done, 1)
                    continue
                if unit == V_X[0]:
                    pe.wait_ge(unit_lo, UNITS.index(X_T[-1]) + 1)
                for c in range(DC):
                    if unit[0] == "v":
                        mm = three(bank[:, unit_bank(u), 0:KV * HD], both(xT, ALL, c, bass.ts(unit[1] - 8, P)),
                                   both(wkv, ALL, c, slice(KV * HD, 2 * KV * HD)), c == 0, c == DC - 1)
                    else:
                        _, j, b = unit
                        rhs = both(ctxT, ALL, c, bass.ts(b, CTX)) if b < B else both(xT, ALL, c, ALL)
                        mm = three(bank[:, unit_bank(u), :], both(wkv, ALL, c, bass.ts(j, P)), rhs, c == 0, c == DC - 1)
                mm.then_inc(unit_done, 1)
                if u in U_Q:
                    misc(U_Q[u])

            def scores(t):
                h, r = tile_at(t)
                b, kv = r // 2, h // G
                if r == 0:
                    pe.wait_ge(misc_free, NM["q", h, 0] + 1)
                if t < 2:
                    pe.wait_ge(unit_lo, NU - 1 + t)
                if t >= 2:
                    pe.wait_ge(exp_done, t - 1)
                s = 2 * (t % 2)
                for o, keys in ((bank[:, s, :], slice(0, 512)), (bank[:, s + 1, 0:KEYS - 512], slice(512, KEYS))):
                    mm = three(o, both(qT, ALL, h % G, bass.ts(r, P)), both(kT, ALL, kv, b, keys), True, True)
                mm.then_inc(scores_done, 1)

            def transposes(t):
                pe.wait_ge(norm_done, t + 1)
                for k in range(2):
                    n = 2 * t + k
                    if n >= 2:
                        pe.wait_ge(pt_lo, n - 1)
                    for j in range(3):
                        mm = pe.transpose(bank[:, 4 + k, bass.ts(j, P)],
                                          prob[:, t % 3, bass.ts(3 * k + j, P)], ident[:, :])
                    mm.then_inc(tr_done, 1)

            def values(p):
                h, r = tile_at(2 * p)
                b, kv = r // 2, h // G
                if p:
                    pe.wait_ge(o_lo, pieces_before(p))
                for j in range(KT):
                    if j % 3 == 0:
                        pe.wait_ge(pt_lo, 2 * (2 * p + 1) + j // 3 + 1)
                    tile = b * KT + j
                    mm = three(bank[0:HD, 6, 0:2 * P], [v[:, tile, kv, 0:HD], v[:, tile, kv, HD:2 * HD]],
                               both(probT, ALL, p % 2, j, ALL), j == 0, j == KT - 1)
                mm.then_inc(pv_done, 1)

            def gate_up(m, cols):
                for k, done in ((0, g_done), (1, u_done)):
                    for c in range(DC):
                        mm = three(bank[:, 4 + 2 * (m % 2) + k, cols], both(wf, ALL, m % 3, bass.ts(4 * k + c, P)),
                                   both(xT, ALL, c, cols), c == 0, c == DC - 1)
                    if cols.stop == ROWS:
                        mm.then_inc(done, 1)

            for it in range(ITERS + 1):
                if it < TILES:
                    scores(it)
                if 0 <= it - TLAG < TILES:
                    transposes(it - TLAG)
                if 0 <= it - PLAG < TILES and (it - PLAG) % 2:
                    values((it - PLAG) // 2)
                for n, item in enumerate(MISC):
                    if item[0] == it:
                        if item[:3] == (ITERS, "x2", RT // B):
                            pe.wait_ge(misc_free, NM["x2", RT // B - 1, 0] + 1)
                            pe.wait_ge(pt_lo, 2 * TILES)
                            pe.wait_ge(wf_lo, 1)
                            gate_up(0, slice(0, ROWS // B))
                        misc(n)

            def down(m):
                pe.wait_ge(h_lo, m + 1)
                for r in range(RT):
                    mm = three(bank[:, r, :], both(hT, ALL, m % 2, bass.ts(r, P)),
                               both(wf, ALL, m % 3, slice(2 * D, FW)), m == 0, m == MT - 1)
                    if m == MT - 1:
                        mm.then_inc(y_done, 1)
                if m < MT - 1:
                    mm.then_inc(y_done, 1)

            for m in range(MT):
                pe.wait_ge(wf_lo, m + 1)
                if m >= 2:
                    pe.wait_ge(h_done, m - 1)
                if m == 0:
                    pe.wait_ge(misc_free, len(MISC))
                gate_up(m, slice(0 if m else ROWS // B, ROWS))
                if m:
                    down(m - 1)
            down(MT - 1)

        @block.scalar
        def _(act):
            for c in range(DC):
                for hi, part, arrived in chunk_parts(c):
                    act.wait_ge(*arrived)
                    act.copy(hi[0], part).then_inc(split_hi, 1)
            act.wait_ge(g_in, 32)
            act.activation(gate_tanh[:, :], gates[:, :], ACT.Tanh).then_inc(tanh_done, 1)

            def misc(n):
                _, kind, i, part = MISC[n]
                if kind in ("wo", "rw"):
                    return
                act.wait_ge(misc_done, n + 1)
                if kind == "q":
                    act.mul(qT[0][:, i % G, :], bank[0:HD, 7, :], SCALE).then_inc(misc_hi, 1)
                else:
                    (hi, _), src = row_place(i)
                    act.copy(hi, src).then_inc(misc_hi, 1)

            def ramp_steps(place):
                for k in MADE.get(place, []):
                    i, j = STEPS[k]
                    if k == STEPS_TO[i]:
                        act.wait_ge(code_at[i % 2], 16 * (i // 2 + 1))
                    if RAMPS <= k < deep:
                        act.wait_ge(ramp_used, k - RAMPS + 1)
                    if k >= deep + DEEP:
                        act.wait_ge(ramp_used, k - DEEP + 1)
                    act.activation(ramp_at(k), code_in[:, i % 2, :], ACT.Relu,
                                   bias=ramp_bias[:, j:j + 1], scale=ramps[j][0]).then_inc(ramp_done, 1)

            def round_wq(h):
                act.wait_ge(wq_in[h % 2], 16 * (h // 2 + 1))
                if h >= 2:
                    act.wait_ge(misc_done, NM["q", h - 2, 0] + 1)
                act.copy(wq[0][:, h % 2], wq_raw[:, h % 2]).then_inc(wq_hi, 1)

            def round_wo(g, c):
                act.wait_ge(wo_in, 16 * (g + 1))
                act.copy(wo[0][:, c, :], wo_raw[:, c, :]).then_inc(wo_hi, 1)

            def load_wf(m):
                if m == 0:
                    act.wait_ge(scores_done, TILES)
                if m >= 2:
                    act.wait_ge(wf_lo, m - 1)
                for s in range(2):
                    act.wait_ge(w_stored[s], 16 * (m + 1))
                act.dma_start(wf_raw[:, m % 2, :], weights[m]).then_inc(wf_in[m % 2], 16)

            def split_wf(m):
                act.wait_ge(wf_in[m % 2], 16 * (m // 2 + 1))
                if m >= 3:
                    act.wait_ge(y_done, m - 2)
                act.copy(wf[0][:, m % 3, :], wf_raw[:, m % 2, :]).then_inc(wf_hi, 1)

            act.wait_ge(zero_done, 1)
            for u, unit in enumerate(UNITS):
                if u == len(V_CTX):
                    round_wq(0)
                    round_wq(1)
                act.wait_ge(unit_done, u + 1)
                for src, hi, _ in unit_places(unit, u):
                    ins = act.copy(hi, src)
                ins.then_inc(unit_hi, 1)
                if u in U_Q:
                    misc(U_Q[u])
                ramp_steps(("unit", u))
            for it in range(ITERS + 1):
                if 0 <= it - TLAG < TILES:
                    t = it - TLAG
                    for k in range(2):
                        act.wait_ge(tr_done, 2 * t + k + 1)
                        if k == 0 and t % 2 == 0 and t >= 4:
                            act.wait_ge(pv_done, t // 2 - 1)
                        (hi, _), src = prob_place(t, k)
                        act.copy(hi, src).then_inc(pt_hi, 1)
                if 0 <= it - PLAG < TILES and (it - PLAG) % 2:
                    p = (it - PLAG) // 2
                    act.wait_ge(pv_done, p + 1)
                    for hi, _, src in pair_places(p):
                        act.copy(hi, src).then_inc(o_hi, 1)
                if it < TILES:
                    act.wait_ge(max_done, it + 1)
                    if it == 0:
                        act.wait_ge(unit_done, NU)
                    if it >= 3:
                        act.wait_ge(tr_done, 2 * (it - 2))
                    s = 2 * (it % 2)
                    act.activation(prob[:, it % 3, :], bank[:, s:s + 2, :].rearrange("p a n -> p (a n)")[:, 0:KEYS],
                                   ACT.Exp, bias=negmax[:, it % 4:it % 4 + 1],
                                   accum_out=rowsum[:, it:it + 1]).then_inc(exp_done, 1)
                if it in WQ_SPLIT:
                    round_wq(WQ_SPLIT[it])
                if it in WO_SPLIT:
                    round_wo(*WO_SPLIT[it])
                ramp_steps(("att", it))
                for n, item in enumerate(MISC):
                    if item[0] == it:
                        misc(n)
                if it == TILES:
                    load_wf(0)
                    load_wf(1)
                if it == TILES + 2:
                    split_wf(0)

            load_wf(2)
            for m in range(MT):
                if m + 1 < MT:
                    split_wf(m + 1)
                act.wait_ge(g_done, m + 1)
                if m >= 2:
                    act.wait_ge(h_done, m - 1)
                act.activation(sg[:, m % 2, :], bank[:, 4 + 2 * (m % 2), :], ACT.Silu, scale=-1.0).then_inc(sg_done, 1)
                ramp_steps(("ffn", m))
                if m + 3 < MT:
                    load_wf(m + 3)

        @block.vector
        def _(dve):
            ln_count = [0]

            def link(ins):
                ln_count[0] += 1
                ins.then_inc(ln_step, 1)
                dve.wait_ge(ln_step, ln_count[0])

            def variances(sl):
                for r in range(RT)[sl]:
                    ln_count[0] += 1
                    dve.bn_stats(stats[:, r, :], xres[:, r, :]).then_inc(ln_step, 1)
                dve.wait_ge(ln_step, ln_count[0])
                for r in range(RT)[sl]:
                    ln_count[0] += 1
                    dve.bn_aggr(meanvar[:, r, :], stats[:, r, :]).then_inc(ln_step, 1)
                dve.wait_ge(ln_step, ln_count[0])
                dve.tensor_scalar(vareps[:, sl], meanvar[:, sl, 1], EPS, None, ALU.add).then_inc(var_done, 1)

            def normalize(sl, n, dst):
                dve.wait_ge(rough_done, n)
                rr = rough[:, sl]
                link(dve.tensor_tensor(newton[:, 0, sl], rr, rr, ALU.mult))
                link(dve.scalar_tensor_tensor(out=newton[:, 1, sl], in0=newton[:, 0, sl], scalar=-0.5,
                                              in1=vareps[:, sl], op0=ALU.mult, op1=ALU.mult))
                link(dve.scalar_tensor_tensor(out=rstd[:, sl], in0=newton[:, 1, sl], scalar=1.5, in1=rr,
                                              op0=ALU.add, op1=ALU.mult))
                for r in range(RT)[sl]:
                    dve.tensor_scalar(dst(r), xres[:, r, :], meanvar[:, r, 0:1], rstd[:, r:r + 1],
                                      ALU.subtract, ALU.mult).then_inc(xhat_done, 1)

            for j, (_, b, _) in enumerate(ramps):
                ins = dve.memset(ramp_bias[:, j:j + 1], b)
            dve.memset(neghalf[:, :], -0.5).then_inc(zero_done, 1)
            for c in range(DC):
                for n, (hi_lo, part, _) in enumerate(chunk_parts(c)):
                    dve.wait_ge(split_hi, 4 * c + n + 1)
                    dve.tensor_tensor(hi_lo[1], part, f32(hi_lo[0]), ALU.subtract).then_inc(split_lo, 1)

            def dequant_steps(place, part=slice(None)):
                for k in SLOTS.get(place, [])[part]:
                    i, j = STEPS[k]
                    dve.wait_ge(ramp_done, k + 1)
                    if k == STEPS_TO[i]:
                        dve.wait_ge(line_step, i + 1)
                    else:
                        dve.wait_ge(ramp_used, k)
                    dve.scalar_tensor_tensor(out=acc[:, i % 2, :], in0=ramp_at(k), scalar=ramps[j][2],
                                             in1=acc[:, i % 2, :], op0=ALU.min, op1=ALU.add).then_inc(ramp_used, 1)

            def misc(n):
                _, kind, i, part = MISC[n]
                if kind in ("wo", "rw"):
                    r = part if kind == "wo" else i
                    if (i, part) == (0, 0):
                        dve.wait_ge(tanh_done, 1)
                    dve.wait_ge(misc_done, n + 1)
                    dve.scalar_tensor_tensor(out=xres[:, r, :], in0=bank[:, 7, :], scalar=gate_tanh[:, 0:1],
                                             in1=xres[:, r, :], op0=ALU.mult, op1=ALU.add).then_inc(misc_free, 1)
                    if kind == "rw":
                        dve.wait_ge(misc_free, n + 1)
                        variances(slice(r, r + 1))
                    return
                dve.wait_ge(misc_hi, Q_HI[n] + 1)
                if kind == "q":
                    dve.scalar_tensor_tensor(out=qT[1][:, i % G, :], in0=bank[0:HD, 7, :], scalar=SCALE,
                                             in1=f32(qT[0][:, i % G, :]), op0=ALU.mult,
                                             op1=ALU.subtract).then_inc(misc_free, 1)
                else:
                    (hi, lo), src = row_place(i)
                    dve.tensor_tensor(lo, src, f32(hi), ALU.subtract).then_inc(misc_free, 1)

            dve.wait_ge(x_in, 16)
            variances(slice(0, RT))
            for u, unit in enumerate(UNITS):
                if u == len(V_CTX):
                    normalize(slice(0, RT), 1, lambda r: xhat[:, r, :])
                dve.wait_ge(unit_hi, u + 1)
                for src, hi, lo in unit_places(unit, u):
                    ins = dve.tensor_tensor(lo, src, f32(hi), ALU.subtract)
                ins.then_inc(unit_lo, 1)
                if u in U_Q:
                    misc(U_Q[u])
                dequant_steps(("unit", u))

            def normalize_row(r):
                if r >= 2:
                    dve.wait_ge(misc_done, NM["x2", r - 2, 0] + 1)
                normalize(slice(r, r + 1), 2 + r, lambda r: xhat2[:, r % 2, :])

            for it in range(ITERS + 1):
                if 0 <= it - 1 < TILES:
                    dve.wait_ge(exp_done, it)
                    dve.reciprocal(rinv[:, it - 1:it], rowsum[:, it - 1:it]).then_inc(rinv_done, 1)
                if it < TILES:
                    s = 2 * (it % 2)
                    dve.wait_ge(scores_done, it + 1)
                    if it >= 4:
                        dve.wait_ge(exp_done, it - 3)
                    dve.tensor_reduce(negmax[:, it % 4:it % 4 + 1],
                                      bank[:, s:s + 2, :].rearrange("p a n -> p (a n)")[:, 0:KEYS],
                                      AX.X, ALU.max, negate=True).then_inc(max_done, 1)
                if 0 <= it - TLAG < TILES:
                    t = it - TLAG
                    for k in range(2):
                        dve.wait_ge(pt_hi, 2 * t + k + 1)
                        (hi, lo), src = prob_place(t, k)
                        dve.tensor_tensor(lo, src, f32(hi), ALU.subtract).then_inc(pt_lo, 1)
                if 0 <= it - PLAG < TILES and (it - PLAG) % 2:
                    p = (it - PLAG) // 2
                    for n, (hi, lo, src) in enumerate(pair_places(p)):
                        dve.wait_ge(o_hi, pieces_before(p) + n + 1)
                        dve.tensor_tensor(lo, src, f32(hi), ALU.subtract).then_inc(o_lo, 1)
                dequant_steps(("att", it))
                for n, item in enumerate(MISC):
                    if item[0] == it:
                        misc(n)
                    if item[1] == "rw" and it == min(item[0] + 1, ITERS):
                        normalize_row(item[2])

            for m in range(MT):
                dequant_steps(("ffn", m), slice(0, 2))
                dve.wait_ge(u_done, m + 1)
                dve.wait_ge(sg_done, m + 1)
                dve.tensor_tensor(hid[:, m % 2, :], bank[:, 5 + 2 * (m % 2), :], sg[:, m % 2, :],
                                  ALU.mult).then_inc(h_done, 1)
                dve.wait_ge(h_done, m + 1)
                if m >= 2:
                    dve.wait_ge(y_done, m - 1)
                dve.tensor_copy(hT[0][:, m % 2, :], hid[:, m % 2, :]).then_inc(h_hi, 1)
                dve.wait_ge(h_hi, m + 1)
                dve.tensor_tensor(hT[1][:, m % 2, :], hid[:, m % 2, :], f32(hT[0][:, m % 2, :]),
                                  ALU.subtract).then_inc(h_lo, 1)
                dequant_steps(("ffn", m), slice(2, None))
            for r in range(RT):
                dve.wait_ge(y_done, MT + r)
                dve.scalar_tensor_tensor(out=result[:, r, :], in0=bank[:, r, :], scalar=gate_tanh[:, 1:2],
                                         in1=xres[:, r, :], op0=ALU.mult, op1=ALU.add).then_inc(res_done, 1)

        @block.gpsimd
        def _(pool):
            pool.memset(ident[:, :], 0.0).then_inc(zero_done, 1)
            pool.wait_ge(zero_done, 2)
            pool.affine_select(out=ident[:, :], in_=ident[:, :], compare_op=ALU.not_equal, fill=1.0, base=0,
                               pattern=[[-1, P]], channel_multiplier=1).then_inc(const_done, 1)

            def rough_power(n, sl):
                pool.wait_ge(var_done, n)
                pool.tensor_tensor(rough[:, sl], vareps[:, sl], neghalf[:, sl], ALU.pow).then_inc(rough_done, 1)

            def line(i):
                pool.wait_ge(code_at[i % 2], 16 * (i // 2 + 1))
                if i >= 2:
                    pool.wait_ge(w_ready, i - 1)
                pool.tensor_scalar(acc[:, i % 2, :], code_in[:, i % 2, :], -slope, offset, ALU.mult,
                                   ALU.add).then_inc(line_step, 1)

            def multiply(place):
                for k in SLOTS.get(place, []):
                    i, _ = STEPS[k]
                    if k == STEPS_TO[i] and i + 1 < CHUNKS:
                        line(i + 1)
                    if k + 1 == STEPS_TO[i + 1]:
                        pool.wait_ge(scale_at[i % 2], 32 * (i // 2 + 1))
                        pool.wait_ge(ramp_used, k + 1)
                        pool.tensor_tensor(scale_in[:, i % 2, :], acc[:, i % 2, :], scale_in[:, i % 2, :],
                                           ALU.mult).then_inc(w_ready, 1)

            def split_wq(h):
                pool.wait_ge(wq_hi, h + 1)
                pool.tensor_tensor(wq[1][:, h % 2], wq_raw[:, h % 2], f32(wq[0][:, h % 2]),
                                   ALU.subtract).then_inc(wq_lo, 1)

            rough_power(1, slice(0, RT))
            split_wq(0)
            split_wq(1)
            line(0)
            for u in range(NU):
                multiply(("unit", u))
            def split_wf(m):
                pool.wait_ge(wf_hi, m + 1)
                pool.tensor_tensor(wf[1][:, m % 3, :], wf_raw[:, m % 2, :], f32(wf[0][:, m % 3, :]),
                                   ALU.subtract).then_inc(wf_lo, 1)

            for it in range(ITERS + 1):
                if 0 <= it - 1 < TILES:
                    pool.wait_ge(rinv_done, it)
                    pool.tensor_tensor(prob[:, (it - 1) % 3, :], prob[:, (it - 1) % 3, :],
                                       rinv[:, it - 1:it].to_broadcast([P, KEYS]), ALU.mult).then_inc(norm_done, 1)
                for item in MISC:
                    if item[1] == "rw" and item[0] == it:
                        rough_power(2 + item[2], slice(item[2], item[2] + 1))
                if it in WQ_SPLIT:
                    split_wq(WQ_SPLIT[it])
                if it in WO_SPLIT:
                    g, c = WO_SPLIT[it]
                    pool.wait_ge(wo_hi, OC * g + c + 1)
                    pool.tensor_tensor(wo[1][:, c, :], wo_raw[:, c, :], f32(wo[0][:, c, :]),
                                       ALU.subtract).then_inc(wo_lo, 1)
                multiply(("att", it))
                if it == TILES + 2:
                    split_wf(0)

            for m in range(MT):
                if m + 1 < MT:
                    split_wf(m + 1)
                multiply(("ffn", m))


def kernel(**inputs):
    import numpy as np
    import concourse.bacc as bacc
    from concourse.bass_utils import run_bass_kernel_spmd

    a = {k: np.asarray(x) for k, x in inputs.items()}

    def tiles_of(w):
        return w.T.reshape(DC, P, MT, P).transpose(2, 1, 0, 3).reshape(MT, P, DC * P)

    def scales_of(s):
        return s.reshape(MT, P, DC, 2).transpose(0, 3, 2, 1).reshape(MT, 2, DC * P)

    def spread(w):
        return np.concatenate([w[..., :OC, :, :], w[..., OC, :, :].reshape(*w.shape[:-3], OC, P - HD, w.shape[-1])],
                              axis=-2)

    arrays = {
        "x": a["x"].reshape(ROWS, D),
        "ctx_t": a["ctx_4096"].reshape(B * CTX, D).T.reshape(DC, P, B * CTX),
        "wkv_t": np.concatenate([spread(a["L0_xattn_Wk"].reshape(KV, HD, D)).reshape(KV * HD, D).T, a["L0_xattn_Wv"].T], axis=1).reshape(DC, P, 2 * KV * HD),
        "wq_t": a["L0_xattn_Wq"].T.reshape(DC, P, H, HD).transpose(2, 1, 0, 3).reshape(H, P, DC * HD),
        "wo_t": spread(a["L0_xattn_Wo"].T.reshape(KV, G, HD, D)).transpose(0, 2, 1, 3).reshape(KV, P, OC * D),
        "codes": np.concatenate([
            tiles_of(a["L0_ffn_gate_q"]), tiles_of(a["L0_ffn_up_q"]),
            a["L0_ffn_down_q"].T.reshape(MT, P, D)], axis=2),
        "absmax": np.concatenate([
            scales_of(a["L0_ffn_gate_absmax"]), scales_of(a["L0_ffn_up_absmax"]),
            a["L0_ffn_down_absmax"].reshape(D, MT, 2).transpose(1, 2, 0)], axis=2),
        "g_xattn": a["g_xattn"].reshape(1, 1),
        "g_ffn": a["g_ffn"].reshape(1, 1),
    }
    nc = bacc.Bacc("TRN2", target_bir_lowering=False, num_devices=1, dynamic_dma_scratch_size=1024)
    arrays = {k: np.ascontiguousarray(x) for k, x in arrays.items()}
    args = [nc.dram_tensor(f"in_{k}", x.shape, mybir.dt.from_np(x.dtype), kind="ExternalInput").ap()
            for k, x in arrays.items()]
    weights = nc.dram_tensor("ffn_weights", (MT, P, FW), F32, kind="Internal").ap()
    out = nc.dram_tensor("out", (ROWS, D), F32, kind="ExternalOutput").ap()
    flamingo_block(nc, *args, weights, out)
    r = run_bass_kernel_spmd(nc, [{f"in_{k}": x for k, x in arrays.items()}], core_ids=[0])
    return r.results[0]["out"].reshape(B, SEQ, D)
```
